# Optimizing a Trainium2 kernel written in Bass

```python
import numpy as np
import jax
import jax.numpy as jnp

def _softmax(x, axis=-1):
    return jax.nn.softmax(x, axis=axis)

def _gelu(x):
    return jax.nn.gelu(x, approximate=True)

def _silu(x):
    return jax.nn.silu(x)

def _sigmoid(x):
    return jax.nn.sigmoid(x)

def _layernorm(x, axis=-1, eps=1e-05):
    m = jnp.mean(x, axis=axis, keepdims=True)
    v = jnp.var(x, axis=axis, keepdims=True)
    return (x - m) / jnp.sqrt(v + eps)

def _scatter_add(tgt, idx, src, axis=0):
    return tgt.at[idx].add(src)

def _segment_sum(src, seg, n):
    return jax.ops.segment_sum(src, seg, n)
kernel_name = 'mk_flamingo_gated_d1_seqx_r4_e6f380'

def setup_inputs(seed: int=0):
    np.random.seed(seed)
    _w = jnp.asarray

    def _rec_inputs():
        import jax
        import jax.numpy as jnp
        _rk = jax.random.key(seed)
        x = -0.0002928 + 1 * jax.random.normal(jax.random.fold_in(_rk, 1), (8, 512, 256), jnp.float32)
        _lenS = 512 - jax.random.randint(jax.random.fold_in(_rk, 7), (8,), 0, max(1, 512 // 4) + 1, jnp.int32)
        _lenS2 = 512 - jax.random.randint(jax.random.fold_in(_rk, 8), (8,), 0, max(1, 512 // 4) + 1, jnp.int32)
        _ctx_1024P = jax.random.normal(jax.random.fold_in(_rk, 11), (8, 16, 256), jnp.float32)
        _ctx_1024c = jax.random.dirichlet(jax.random.fold_in(_rk, 511), 0.3 * jnp.ones((16,), jnp.float32), (8, 512))
        _ctx_1024t = jnp.einsum('bsk,bkd->bsd', _ctx_1024c, _ctx_1024P)
        _ctx_1024t = _ctx_1024t * jax.lax.rsqrt(jnp.mean(jnp.square(_ctx_1024t)) + 1e-12) * 0.953939
        ctx_1024 = -1.39393e-06 + 0.999914 * (_ctx_1024t + 0.3 * jax.random.normal(jax.random.fold_in(_rk, 611), (8, 512, 256), jnp.float32))
        _g = jax.random.normal(jax.random.fold_in(_rk, 9001), (2, 1), jnp.float32)
        _g = jnp.sign(_g) * jnp.maximum(jnp.abs(_g), 1.0) + (_g == 0) * 1.0
        g_xattn = _g[0]
        g_ffn = _g[1]
        return (x, ctx_1024, g_xattn, g_ffn)
    x, ctx_1024, g_xattn, g_ffn = _rec_inputs()

    def _L0_xattn_setup():
        import jax, jax.numpy as jnp
        import numpy as np
        B, S, D, NH = (2, 512, 256, 8)
        DH = D // NH
        EPS = 1e-06
        LN_EPS = 1e-05

        def _mlstm_cell(q, k, v, igate_w, igate_b, fgate_w, fgate_b, ln_scale):
            Slen = q.shape[0]
            ifg = jnp.concatenate([q, k, v], axis=-1)
            ig = (ifg @ igate_w.T + igate_b).T
            fg = (ifg @ fgate_w.T + fgate_b).T
            qh = q.reshape(Slen, NH, DH).transpose(1, 0, 2)
            kh = k.reshape(Slen, NH, DH).transpose(1, 0, 2)
            vh = v.reshape(Slen, NH, DH).transpose(1, 0, 2)
            log_f = jax.nn.log_sigmoid(fg)
            cs = jnp.cumsum(log_f, axis=1)
            fg_mat = cs[:, :, None] - cs[:, None, :]
            mask = jnp.tril(jnp.ones((Slen, Slen), dtype=bool))
            log_fg_mat = jnp.where(mask, fg_mat, -jnp.inf)
            log_D = log_fg_mat + ig[:, None, :]
            max_log_D = jnp.max(log_D, axis=-1, keepdims=True)
            D_mat = jnp.exp(log_D - max_log_D)
            qk = jnp.einsum('hsd,htd->hst', qh, kh) / np.sqrt(DH)
            C = qk * D_mat
            normalizer = jnp.maximum(jnp.abs(C.sum(axis=-1, keepdims=True)), jnp.exp(-max_log_D))
            h = jnp.einsum('hst,htd->hsd', C / (normalizer + EPS), vh)
            h = h.transpose(1, 0, 2).reshape(Slen, D)
            mu = h.mean(axis=-1, keepdims=True)
            var = h.var(axis=-1, keepdims=True)
            return (h - mu) / jnp.sqrt(var + LN_EPS) * ln_scale
        key = jax.random.key(seed)
        ks = jax.random.split(key, 8)
        rnd = lambda k, sh, s=1.0: jax.random.normal(k, sh, dtype=jnp.float32) * s
        return {'q': rnd(ks[0], (B, S, D)), 'k': rnd(ks[1], (B, S, D)), 'v': rnd(ks[2], (B, S, D)), 'igate_w': rnd(ks[3], (NH, 3 * D), 0.02), 'igate_b': jnp.linspace(3.0, 6.0, NH, dtype=jnp.float32), 'fgate_w': rnd(ks[4], (NH, 3 * D), 0.02), 'fgate_b': rnd(ks[5], (NH,), 0.3162278), 'ln_scale': jnp.ones((D,), dtype=jnp.float32)}
    _L0_xattn_all = _L0_xattn_setup()
    _L0_xattn_in = {k: v for k, v in _L0_xattn_all.items() if k in ('igate_w', 'igate_b', 'fgate_w', 'fgate_b', 'ln_scale')}
    del _L0_xattn_all

    def _L0_ffn_setup():
        import jax, jax.numpy as jnp
        import numpy as np
        TOP_K = 2
        ROUTE_SCALE = 1.0
        EPS = 1e-20
        key = jax.random.key(seed)
        ks = jax.random.split(key, 8)
        dim, hid, E, X = (256, 704, 8, 1)
        std = 0.02
        x = jax.random.normal(ks[0], (2, 512, dim), dtype=jnp.float32)
        w1 = jax.random.normal(ks[1], (E, hid, dim), dtype=jnp.float32) * std
        w2 = jax.random.normal(ks[2], (E, dim, hid), dtype=jnp.float32) * std
        w3 = jax.random.normal(ks[3], (E, hid, dim), dtype=jnp.float32) * std
        new_w1 = jax.random.normal(ks[4], (X, hid, dim), dtype=jnp.float32) * std
        new_w2 = jnp.zeros((X, dim, hid), dtype=jnp.float32)
        new_w3 = jax.random.normal(ks[5], (X, hid, dim), dtype=jnp.float32) * std
        gate_weight = jax.random.normal(ks[6], (E, dim), dtype=jnp.float32) * std
        new_gate_weight = jax.random.normal(ks[7], (X, dim), dtype=jnp.float32) * std
        gate_bias = jnp.zeros((X,), dtype=jnp.float32)
        return dict(x=x, w1=w1, w2=w2, w3=w3, new_w1=new_w1, new_w2=new_w2, new_w3=new_w3, gate_weight=gate_weight, new_gate_weight=new_gate_weight, gate_bias=gate_bias)
    _L0_ffn_all = _L0_ffn_setup()
    _L0_ffn_in = {k: v for k, v in _L0_ffn_all.items() if k in ('w1', 'w2', 'w3', 'new_w1', 'new_w2', 'new_w3', 'gate_weight', 'new_gate_weight', 'gate_bias')}
    del _L0_ffn_all
    return {'x': x, 'ctx_1024': ctx_1024, 'g_xattn': g_xattn, 'g_ffn': g_ffn, 'L0_xattn_igate_w': _L0_xattn_in['igate_w'], 'L0_xattn_igate_b': _L0_xattn_in['igate_b'], 'L0_xattn_fgate_w': _L0_xattn_in['fgate_w'], 'L0_xattn_fgate_b': _L0_xattn_in['fgate_b'], 'L0_xattn_ln_scale': _L0_xattn_in['ln_scale'], 'L0_ffn_w1': _L0_ffn_in['w1'], 'L0_ffn_w2': _L0_ffn_in['w2'], 'L0_ffn_w3': _L0_ffn_in['w3'], 'L0_ffn_new_w1': _L0_ffn_in['new_w1'], 'L0_ffn_new_w2': _L0_ffn_in['new_w2'], 'L0_ffn_new_w3': _L0_ffn_in['new_w3'], 'L0_ffn_gate_weight': _L0_ffn_in['gate_weight'], 'L0_ffn_new_gate_weight': _L0_ffn_in['new_gate_weight'], 'L0_ffn_gate_bias': _L0_ffn_in['gate_bias']}

def reference(x, ctx_1024, g_xattn, g_ffn, L0_xattn_igate_w, L0_xattn_igate_b, L0_xattn_fgate_w, L0_xattn_fgate_b, L0_xattn_ln_scale, L0_ffn_w1, L0_ffn_w2, L0_ffn_w3, L0_ffn_new_w1, L0_ffn_new_w2, L0_ffn_new_w3, L0_ffn_gate_weight, L0_ffn_new_gate_weight, L0_ffn_gate_bias):
    import jax
    import jax.numpy as jnp

    def _L0_xattn_ref(q, k, v, igate_w, igate_b, fgate_w, fgate_b, ln_scale):
        import jax, jax.numpy as jnp
        import numpy as np
        B, S, D, NH = (2, 512, 256, 8)
        DH = D // NH
        EPS = 1e-06
        LN_EPS = 1e-05

        def _mlstm_cell(q, k, v, igate_w, igate_b, fgate_w, fgate_b, ln_scale):
            Slen = q.shape[0]
            ifg = jnp.concatenate([q, k, v], axis=-1)
            ig = (ifg @ igate_w.T + igate_b).T
            fg = (ifg @ fgate_w.T + fgate_b).T
            qh = q.reshape(Slen, NH, DH).transpose(1, 0, 2)
            kh = k.reshape(Slen, NH, DH).transpose(1, 0, 2)
            vh = v.reshape(Slen, NH, DH).transpose(1, 0, 2)
            log_f = jax.nn.log_sigmoid(fg)
            cs = jnp.cumsum(log_f, axis=1)
            fg_mat = cs[:, :, None] - cs[:, None, :]
            mask = jnp.tril(jnp.ones((Slen, Slen), dtype=bool))
            log_fg_mat = jnp.where(mask, fg_mat, -jnp.inf)
            log_D = log_fg_mat + ig[:, None, :]
            max_log_D = jnp.max(log_D, axis=-1, keepdims=True)
            D_mat = jnp.exp(log_D - max_log_D)
            qk = jnp.einsum('hsd,htd->hst', qh, kh) / np.sqrt(DH)
            C = qk * D_mat
            normalizer = jnp.maximum(jnp.abs(C.sum(axis=-1, keepdims=True)), jnp.exp(-max_log_D))
            h = jnp.einsum('hst,htd->hsd', C / (normalizer + EPS), vh)
            h = h.transpose(1, 0, 2).reshape(Slen, D)
            mu = h.mean(axis=-1, keepdims=True)
            var = h.var(axis=-1, keepdims=True)
            return (h - mu) / jnp.sqrt(var + LN_EPS) * ln_scale
        return jax.vmap(lambda qq, kk, vv: _mlstm_cell(qq, kk, vv, igate_w, igate_b, fgate_w, fgate_b, ln_scale))(q, k, v)

    def _L0_ffn_ref(x, w1, w2, w3, new_w1, new_w2, new_w3, gate_weight, new_gate_weight, gate_bias):
        import jax, jax.numpy as jnp
        import numpy as np
        TOP_K = 2
        ROUTE_SCALE = 1.0
        EPS = 1e-20
        bs, slen, dim = x.shape
        x_flat = x.reshape(-1, dim)
        ew1 = jnp.concatenate([w1, new_w1], axis=0)
        ew2 = jnp.concatenate([w2, new_w2], axis=0)
        ew3 = jnp.concatenate([w3, new_w3], axis=0)
        gate = jnp.concatenate([gate_weight, new_gate_weight], axis=0)
        e_orig = w1.shape[0]
        e_tot = gate.shape[0]
        bias = jnp.concatenate([jnp.zeros((e_orig,), x.dtype), gate_bias])
        scores = jax.nn.sigmoid((x_flat @ gate.T + bias).astype(jnp.float32))
        top_scores, selected = jax.lax.top_k(scores, TOP_K)
        top_scores = top_scores / (jnp.sum(top_scores, axis=-1, keepdims=True) + EPS)
        top_scores = top_scores * ROUTE_SCALE
        onehot = jax.nn.one_hot(selected, e_tot, dtype=jnp.float32)
        cw = jnp.einsum('tk,tke->te', top_scores, onehot)
        out = jnp.zeros_like(x_flat)
        for e in range(e_tot):
            h = jax.nn.silu(x_flat @ ew1[e].T) * (x_flat @ ew3[e].T)
            out = out + cw[:, e:e + 1] * (h @ ew2[e].T)
        return out.reshape(bs, slen, dim)
    x = x + jnp.tanh(g_xattn[0]) * _L0_xattn_ref(_layernorm(x, axis=-1), ctx_1024, ctx_1024, L0_xattn_igate_w, L0_xattn_igate_b, L0_xattn_fgate_w, L0_xattn_fgate_b, L0_xattn_ln_scale)
    x = x + jnp.tanh(g_ffn[0]) * _L0_ffn_ref(_layernorm(x, axis=-1), L0_ffn_w1, L0_ffn_w2, L0_ffn_w3, L0_ffn_new_w1, L0_ffn_new_w2, L0_ffn_new_w3, L0_ffn_gate_weight, L0_ffn_new_gate_weight, L0_ffn_gate_bias)
    return x

_drawn_inputs = setup_inputs


def setup_inputs(seed=0):
    import zlib

    import numpy as np

    out = dict(_drawn_inputs(seed))
    spreads = {'L0_xattn_ln_scale': (1.0, 0.2), 'L0_ffn_new_w2': (0.0, 0.371)}
    factors = {'L0_ffn_w1': 4.407,
     'L0_ffn_w2': 4.236,
     'L0_ffn_w3': 4.247,
     'L0_ffn_gate_weight': 3.24,
     'L0_ffn_new_gate_weight': 2.992}
    for name, (base, spread) in spreads.items():
        noise = np.random.default_rng([zlib.crc32(name.encode()), seed]).standard_normal(out[name].shape)
        drawn = base * np.exp(spread * noise) if base else spread * noise
        out[name] = jnp.asarray(drawn.astype(out[name].dtype))
    for name, factor in factors.items():
        out[name] = (out[name] * factor).astype(out[name].dtype)
    return out
```

```python
from contextlib import ExitStack

import concourse.bass as bass
from concourse import mybir

ALU = mybir.AluOpType
ACT = mybir.ActivationFunctionType
AX = mybir.AxisListType
F32 = mybir.dt.float32
BF16 = mybir.dt.bfloat16
I32 = mybir.dt.int32
U32 = mybir.dt.uint32

P = 128
NB, S, D, NH = 8, 512, 256, 8
DH = D // NH
DV = DH + 1
NC = S // P
NT = NB * NC
BH = NB * NH
TOK = NB * S
NE, HID, TOPK = 9, 704, 2
KD = D // P
HG = 4
NM = 6
HREM = HID - 5 * P
W13 = KD * 2 * HID
W2C = NM * D
WE = W13 + W2C
WALL = NE * WE
WCH = WALL // NT
SLOT = 256
SLOTS = (TOK * TOPK + NE * (SLOT - 1)) // SLOT
NQ = SLOTS * SLOT // P
YW = D + 16
SKIP = 8192.0
LN_EPS, N_EPS, TOP_EPS = 1e-5, 1e-6, 1e-20
SCALE = float(1.0 / DH ** 0.5)
NEG = -1e30


def build(nc, x, kv, wgate, ifb, lnrow, gsc, wroute, rbias, wts, out):
    with ExitStack() as ctx:
        def sb(name, shape, dt=F32):
            return ctx.enter_context(nc.sbuf_tensor(name, shape, dt))

        def sem(name):
            return ctx.enter_context(nc.semaphore(name))

        def dram(name, shape, dt):
            return nc.dram_tensor(name, shape, dt, kind="Internal").ap()

        qT_d = dram("qT_d", [NT, P, D], F32)
        am_d = dram("am_d", [NB, 3 * NH, 2, S], BF16)
        whi_d = dram("whi_d", [P, WALL], BF16)
        wlo_d = dram("wlo_d", [P, WALL], BF16)
        y_d = dram("y_d", [TOK, YW], F32)

        bank = ctx.enter_context(nc.psum_tensor("bank", [P, 8, 512], F32))

        rowj = sb("rowj", [P, P]); pcol = sb("pcol", [P, 1]); blk = sb("blk", [P, HG * DV])
        tokp1 = sb("tokp1", [P, NT])
        identf = sb("identf", [P, P]); identb = sb("identb", [P, P], BF16)
        upperb = sb("upperb", [P, P], BF16); onesb = sb("onesb", [P, P], BF16)
        maskb = sb("maskb", [P, P], BF16); sel24 = sb("sel24", [24, NH], BF16)
        selt = sb("selt", [24, NH]); blkm = sb("blkm", [P, HG * DV]); blkt = sb("blkt", [P, HG * DV])
        eps_c = sb("eps_c", [P, 1]); one_c = sb("one_c", [P, 1]); neps = sb("neps", [P, 1])
        ones_row = sb("ones_row", [P, S])
        wg = sb("wg", [P, 6, 2 * NH]); wgkv = sb("wgkv", [P, 2, 2 * NH]); ifb_s = sb("ifb_s", [BH, 2])
        lnr = sb("lnr", [P, D]); gs = sb("gs", [P, 2]); tg = sb("tg", [P, 2]); lsg = sb("lsg", [P, D])
        wr = sb("wr", [P, KD, NE]); rb = sb("rb", [P, NE])

        col = sb("col", [P, NT, 3 * NH + 2])
        kvb = [sb(f"kvb{c}", [P, D + NH * DV]) for c in range(NC)]
        qtb = [sb(f"qtb{c}", [P, D]) for c in range(NC)]
        qbd = [sb(f"qbd{c}", [P, 2, HG, P]) for c in range(NC)]
        amb = [sb(f"amb{c}", [24, 2, P], BF16) for c in range(NC)]
        colb = [sb(f"colb{c}", [P, 3 * NH + 2]) for c in range(NC)]
        Dm = [sb(f"Dm{g}", [P, 512]) for g in range(2)]
        Cm = [sb(f"Cm{g}", [P, 512]) for g in range(2)]
        kw = sb("kw", [P, D]); St = sb("St", [P, 2, HG * DV]); Sd = sb("Sd", [P, 2, HG * DV])
        Ut = sb("Ut", [P, 2, HG * DV])
        t1 = sb("t1", [P, NH, DV]); Hs = sb("Hs", [P, NH, DV])
        n1 = sb("n1", [P, NH]); n2 = sb("n2", [P, NH]); n3 = sb("n3", [P, NH])
        h = sb("h", [P, NC, D])
        wst = [sb(f"wst{w}", [P, WCH]) for w in range(2)]
        wh = [sb(f"wh{w}", [P, WCH], BF16) for w in range(2)]
        wl = [sb(f"wl{w}", [P, WCH], BF16) for w in range(2)]
        xc = sb("xc", [P, NC, D]); st2 = sb("st2", [P, NC, 6]); mv2 = sb("mv2", [P, NC, 2])
        lv2 = sb("lv2", [P, NC]); rs2 = sb("rs2", [P, NC]); hn = sb("hn", [P, NC, D]); hl = sb("hl", [P, NC, D])
        x2 = sb("x2", [P, NC, D])
        st3 = sb("st3", [P, NC, 6]); mv3 = sb("mv3", [P, NC, 2]); lv3 = sb("lv3", [P, NC]); rs3 = sb("rs3", [P, NC])
        y = sb("y", [P, NC, D]); yT = sb("yT", [P, NC, KD, P]); lg = sb("lg", [P, NT, NE])

        early_ctx = ExitStack()

        def early(name, shape, dt=F32):
            return early_ctx.enter_context(nc.sbuf_tensor(name, shape, dt))

        xa = [early(f"xa{u}", [P, D]) for u in range(8)]
        ka = [early(f"ka{u}", [P, D]) for u in range(8)]
        stA = early("stA", [P, 8, 6]); mvA = early("mvA", [P, 8, 2]); lvA = early("lvA", [P, 8]); rsA = early("rsA", [P, 8])
        qn = [early(f"qn{u}", [P, D]) for u in range(8)]
        qt = [early(f"qt{u}", [P, D]) for u in range(8)]
        gall = early("gall", [P, NC, 2, NB, NH])
        z = early("z", [BH, S]); g1 = early("g1", [BH, S]); g2 = early("g2", [BH, S]); g3 = early("g3", [BH, S])
        lf = early("lf", [BH, S]); cs = early("cs", [BH, S]); ga = early("ga", [BH, S]); gm = early("gm", [BH, S])
        r1 = early("r1", [BH, S]); r2 = early("r2", [BH, S])
        ap = [early(f"ap{k}", [BH, S], BF16) for k in range(3)]
        mp = [early(f"mp{k}", [BH, S], BF16) for k in range(3)]
        gw = early("gw", [BH, S]); gE = early("gE", [BH, S]); gn = early("gn", [BH, S]); gd = early("gd", [BH, NC])
        gdx = early("gdx", [BH, NC]); spread = early("spread", [BH, BH * DH])
        early_ctx.close()

        s_iota = sem("s_iota"); s_const = sem("s_const"); s_small = sem("s_small"); s_tanh = sem("s_tanh")
        s_qz = sem("s_qz"); s_wgkv = sem("s_wgkv"); s_lsg = sem("s_lsg")
        a_x = [sem(f"a_x{u}") for u in range(8)]; a_k = [sem(f"a_k{u}") for u in range(8)]
        a_st = sem("a_st"); a_mv = sem("a_mv"); a_lv = sem("a_lv"); a_rs = sem("a_rs"); a_q = sem("a_q")
        a_tr = sem("a_tr"); a_qt = sem("a_qt"); a_gp = sem("a_gp"); a_gs = sem("a_gs")
        a_qo = [sem(f"a_qo{u}") for u in range(8)]
        g_tp = sem("g_tp"); g_act = sem("g_act"); g_dve = sem("g_dve"); g_am = sem("g_am"); g_col = sem("g_col")
        g_dec = sem("g_dec"); g_cols = sem("g_cols")
        b_kv = [sem(f"b_kv{c}") for c in range(NC)]; b_q = [sem(f"b_q{c}") for c in range(NC)]
        b_am = [sem(f"b_am{c}") for c in range(NC)]; b_col = sem("b_col")
        b_dl = sem("b_dl"); b_s = sem("b_s"); b_D = sem("b_D"); b_C = sem("b_C")
        b_kw = sem("b_kw"); b_u = sem("b_u"); b_ut = sem("b_ut"); b_st = sem("b_st"); b_hi = sem("b_hi")
        b_t1 = sem("b_t1"); b_h = sem("b_h"); b_hs = sem("b_hs"); b_n = sem("b_n"); b_ho = sem("b_ho")
        b_sd = sem("b_sd")
        w_in = [sem(f"w_in{w}") for w in range(2)]; w_hi = sem("w_hi"); w_lo = sem("w_lo")
        w_out = [sem(f"w_out{w}") for w in range(2)]
        c_x = sem("c_x"); c_st2 = sem("c_st2"); c_mv2 = sem("c_mv2"); c_lv2 = sem("c_lv2"); c_rs2 = sem("c_rs2")
        c_hn = sem("c_hn"); c_hl = sem("c_hl"); c_x2 = sem("c_x2"); c_st3 = sem("c_st3"); c_mv3 = sem("c_mv3")
        c_lv3 = sem("c_lv3"); c_rs3 = sem("c_rs3"); c_y = sem("c_y"); c_yT = sem("c_yT"); c_yc = sem("c_yc")
        c_lp = sem("c_lp"); c_lg = sem("c_lg"); c_x2o = sem("c_x2o"); c_yo = sem("c_yo")
        s_pace = sem("s_pace")

        def fence(eng):
            eng.sem_inc(s_pace, 1)

        def ge(eng, sem, val):
            if isinstance(val, int):
                if val > 0:
                    eng.wait_ge(sem, val)
                return
            eng.wait_ge(sem, val)
            if eng.engine in (nc.sync.engine, nc.gpsimd.engine):
                fence(eng)

        xv = x.rearrange("(t p) d -> t p d", p=P)
        ov = out.rearrange("(b c p) d -> b p c d", p=P, c=NC)
        xb_v = x.rearrange("(b c p) d -> b p c d", p=P, c=NC)
        yv = y_d.rearrange("(b c p) d -> b p c d", p=P, c=NC)

        def row(v, i, n=1):
            return v[bass.ds(i, n)].rearrange("o p d -> (o p) d")

        def consts_pool(pool):
            nc.gpsimd.iota(rowj[:, :], [[1, P]], base=0, channel_multiplier=0,
                           allow_small_or_imprecise_dtypes=True).then_inc(s_iota, 1)
            nc.gpsimd.iota(pcol[:, :], [[1, 1]], base=0, channel_multiplier=1,
                           allow_small_or_imprecise_dtypes=True).then_inc(s_iota, 1)
            nc.gpsimd.iota(blk[:, :].rearrange("p (h e) -> p h e", e=DV), [[DH, HG], [0, DV]], base=0,
                           channel_multiplier=0, allow_small_or_imprecise_dtypes=True).then_inc(s_iota, 1)
            nc.gpsimd.iota(tokp1[:, :], [[P, NT]], base=1, channel_multiplier=1,
                           allow_small_or_imprecise_dtypes=True).then_inc(s_iota, 1)

        NCONST = 15

        def consts_dve(dve):
            nc.vector.memset(eps_c[:, :], LN_EPS).then_inc(s_const, 1)
            nc.vector.memset(one_c[:, :], 1.0).then_inc(s_const, 1)
            nc.vector.memset(neps[:, :], N_EPS).then_inc(s_const, 1)
            nc.vector.memset(ones_row[:, :], 1.0).then_inc(s_const, 1)
            nc.vector.memset(onesb[:, :], 1.0).then_inc(s_const, 1)
            dve.wait_ge(s_iota, 4)
            nc.vector.tensor_scalar(identf[:, :], rowj[:, :], pcol[:, 0:1], None, ALU.is_equal).then_inc(s_const, 1)
            nc.vector.tensor_scalar(identb[:, :], rowj[:, :], pcol[:, 0:1], None, ALU.is_equal).then_inc(s_const, 1)
            nc.vector.tensor_scalar(upperb[:, :], rowj[:, :], pcol[:, 0:1], None, ALU.is_gt).then_inc(s_const, 1)
            nc.vector.tensor_scalar(maskb[:, :], rowj[:, :], pcol[:, 0:1], NEG, ALU.is_lt, ALU.mult).then_inc(s_const, 1)
            nc.vector.tensor_scalar(blkt[:, :], blk[:, :], float(DH), pcol[:, 0:1], ALU.add, ALU.is_gt).then_inc(s_const, 1)
            nc.vector.tensor_scalar(blkm[:, :], blk[:, :], pcol[:, 0:1], None, ALU.is_le).then_inc(s_const, 1)
            dve.wait_ge(s_const, 11)
            nc.vector.tensor_tensor(blkm[:, :], blkm[:, :], blkt[:, :], ALU.mult).then_inc(s_const, 1)
            nc.vector.tensor_tensor(selt[:, :], identf[0:24, 0:8], identf[0:24, 8:16], ALU.add).then_inc(s_const, 1)
            dve.wait_ge(s_const, 13)
            nc.vector.tensor_tensor(sel24[:, :], selt[:, :], identf[0:24, 16:24], ALU.add).then_inc(s_const, 1)
            nc.vector.tensor_copy(spread[:, :].rearrange("p (b d) -> p b d", d=DH),
                                  identf[0:BH, 0:BH].unsqueeze(2).to_broadcast([BH, BH, DH])).then_inc(s_const, 1)
            dve.wait_ge(s_small, 16 * 6)
            nc.vector.tensor_tensor(wgkv[:, :, :], wg[:, 2:4, :], wg[:, 4:6, :], ALU.add).then_inc(s_wgkv, 1)
            dve.wait_ge(s_tanh, 1)
            nc.vector.tensor_scalar(lsg[:, :], lnr[:, :], tg[:, 0:1], None, ALU.mult).then_inc(s_lsg, 1)

            for c in range(NC):
                nc.vector.memset(qbd[c][:, :, :, :], 0.0).then_inc(s_qz, 1)

        def consts_act(act):
            act.wait_ge(s_small, 16 * 6)
            nc.scalar.activation(tg[:, :], gs[:, :], ACT.Tanh).then_inc(s_tanh, 1)

        def a_sync(sp, i):
            for u in range(8):
                ge(sp, a_q, i * 8 + (u - 7))
                ge(sp, a_gp, i * 8 + (u - 7))
                sp.dma_start(xa[u][:, :], row(xv, i * 8 + u)).then_inc(a_x[u], 16)
                sp.dma_start(ka[u][:, :], row(kv, i * 8 + u)[:, 0:D]).then_inc(a_k[u], 16)

        def a_dve(dve, i):
            for u in range(8):
                ge(dve, a_x[u], i * 16 + 16)
                nc.vector.bn_stats(stA[:, u, :], xa[u][:, :]).then_inc(a_st, 1)
            ge(dve, a_st, i * 8 + 8)
            fence(dve)
            for u in range(8):
                nc.vector.bn_aggr(mvA[:, u, :], stA[:, u, :]).then_inc(a_mv, 1)
            ge(dve, a_rs, i + 1)
            for u in range(8):
                ge(dve, a_tr, i * 8 + (u - 7))
                nc.vector.tensor_scalar(qn[u][:, :], xa[u][:, :], mvA[:, u, 0:1], rsA[:, u:u + 1],
                                        ALU.subtract, ALU.mult).then_inc(a_q, 1)
            for u in range(8):
                ge(dve, a_gp, i * 8 + (u + 1))
                dst = gall[:, u % NC, :, bass.ds(i * 2 + u // NC, 1), :].rearrange("p i o h -> p i (o h)")
                nc.vector.tensor_copy(dst, bank[:, 2 + u % 2, 0:2 * NH].rearrange("p (i h) -> p i h", i=2)).then_inc(a_gs, 1)

        def a_act(act, i):
            ge(act, a_mv, i * 8 + 8)
            nc.scalar.activation(lvA[:, :], mvA[:, :, 1], ACT.Ln, bias=eps_c[:, 0:1]).then_inc(a_lv, 1)
            ge(act, a_lv, i + 1)
            nc.scalar.activation(rsA[:, :], lvA[:, :], ACT.Exp, scale=-0.5).then_inc(a_rs, 1)
            for u in range(8):
                ge(act, a_tr, i * 8 + (u + 1))
                ge(act, a_qo[u], i * 16)
                nc.scalar.copy(qt[u][:, :], bank[:, u % 2, 0:D]).then_inc(a_qt, 1)
                if u:
                    a_store(act, i, u - 1)
            a_store(act, i, 7)

        def a_store(act, i, u):
            ge(act, a_qt, i * 8 + (u + 1))
            act.dma_start(row(qT_d, i * 8 + u), qt[u][:, :]).then_inc(a_qo[u], 16)

        def a_pe_gates(pe, i, u):
            ge(pe, a_qt, i * 8 + (u + 1))
            ge(pe, a_k[u], i * 16 + 16)
            ge(pe, a_gs, i * 8 + (u - 1))
            for k in range(KD):
                nc.tensor.matmul(bank[:, 2 + u % 2, 0:2 * NH], qt[u][:, k * P:(k + 1) * P], wg[:, k, :],
                                 start=(k == 0), stop=False)
            for k in range(KD):
                mm = nc.tensor.matmul(bank[:, 2 + u % 2, 0:2 * NH], ka[u][:, k * P:(k + 1) * P], wgkv[:, k, :],
                                      start=False, stop=(k == KD - 1))
            mm.then_inc(a_gp, 1)

        def a_pe(pe, i):
            for u in range(8):
                ge(pe, a_q, i * 8 + (u + 1))
                ge(pe, a_qt, i * 8 + (u - 1))
                for k in range(KD):
                    mm = nc.tensor.transpose(bank[:, u % 2, k * P:(k + 1) * P], qn[u][:, k * P:(k + 1) * P], identf[:, :])
                mm.then_inc(a_tr, 1)
                if u:
                    a_pe_gates(pe, i, u - 1)
            a_pe_gates(pe, i, 7)

        def ends(t):
            return t[:, :].rearrange("p (c s) -> p c s", c=NC)[:, :, P - 1:P]

        def g_actf_all(act):
            act.wait_ge(g_tp, 1)
            nc.scalar.activation(z[:, :], bank[0:BH, 5, :], ACT.Identity, bias=ifb_s[:, 1:2]).then_inc(g_act, 1)
            act.wait_ge(g_dve, 1)
            nc.scalar.activation(g2[:, :], g1[:, :], ACT.Exp).then_inc(g_act, 1)
            act.wait_ge(g_act, 2)
            nc.scalar.activation(g3[:, :], g2[:, :], ACT.Ln, bias=one_c[0:BH, 0:1]).then_inc(g_act, 1)
            act.wait_ge(g_dve, 11)
            nc.scalar.activation(gw[:, :], g1[:, :], ACT.Exp).then_inc(g_act, 1)
            nc.scalar.activation(gE[:, :], g2[:, :], ACT.Exp).then_inc(g_act, 1)
            nc.scalar.activation(gn[:, :], g3[:, :], ACT.Exp, scale=-1.0).then_inc(g_act, 1)
            nc.scalar.activation(gdx[:, :], gd[:, :], ACT.Exp).then_inc(g_act, 1)
            act.wait_ge(g_col, 1)
            for k in range(3):
                src = bank[:, (6, 7, 2)[k], 0:NC * BH].rearrange("p (c b h) -> p b c h", c=NC, b=NB)
                dst = col[:, :, k * NH:(k + 1) * NH].rearrange("p (b c) h -> p b c h", b=NB)
                if k < 2:
                    nc.scalar.copy(dst, src).then_inc(g_cols, 1)
                else:
                    nc.scalar.activation(dst, src, ACT.Identity, bias=neps[:, 0:1]).then_inc(g_cols, 1)
            act.wait_ge(g_dec, 1)
            nc.scalar.copy(col[:, :, 3 * NH:3 * NH + 2].rearrange("p (b c) k -> p b c k", b=NB),
                           bank[:, 3, 0:2 * NB * NC].rearrange("p (b k c) -> p b c k", b=NB, k=2)).then_inc(g_cols, 1)

        def g_pe_all(pe):
            pe.wait_ge(a_gs, NT)
            for k in range(2):
                for c in range(NC):
                    mm = nc.tensor.transpose(bank[0:BH, 4 + k, c * P:(c + 1) * P],
                                             gall[:, c, k, :, :].rearrange("p b h -> p (b h)"), identf[:, :])
            mm.then_inc(g_tp, 1)
            pe.wait_ge(g_act, 7)
            for k, src in enumerate((gw, gE, gn)):
                for c in range(NC):
                    mm = nc.tensor.transpose(bank[:, (6, 7, 2)[k], c * BH:(c + 1) * BH], src[:, c * P:(c + 1) * P],
                                             identf[0:BH, 0:BH])
            mm.then_inc(g_col, 1)
            for n in range(2 * NB):
                mm = nc.tensor.matmul(bank[:, 3, n * NC:(n + 1) * NC], spread[:, n * P:(n + 1) * P], gdx[:, :], start=True, stop=True)
            mm.then_inc(g_dec, 1)
            pe.wait_ge(g_cols, 4)

        def g_dvef(dve):
            V = nc.vector
            dve.wait_ge(g_act, 1)
            V.scalar_tensor_tensor(g1[:, :], z[:, :], -1.0, z[:, :], ALU.mult, ALU.min).then_inc(g_dve, 1)
            dve.wait_ge(g_act, 3)
            V.scalar_tensor_tensor(lf[:, :], z[:, :], 0.0, g3[:, :], ALU.min, ALU.subtract).then_inc(g_dve, 1)
            dve.wait_ge(g_dve, 2)
            V.tensor_tensor_scan(cs[:, :], ones_row[0:BH, :], lf[:, :], 0.0, ALU.mult, ALU.add).then_inc(g_dve, 1)
            dve.wait_ge(g_dve, 3)
            V.scalar_tensor_tensor(ga[:, :], bank[0:BH, 4, :], ifb_s[:, 0:1], cs[:, :], ALU.add,
                                   ALU.subtract).then_inc(g_dve, 1)
            dve.wait_ge(g_dve, 4)
            V.tensor_tensor_scan(gm[:, :], ga[:, :], ga[:, :], -3e38, ALU.max, ALU.max).then_inc(g_dve, 1)
            dve.wait_ge(g_dve, 5)
            c4 = lambda t: t[:, :].rearrange("p (c s) -> p c s", c=NC)
            m_end = ends(gm)
            V.tensor_tensor(c4(g1), c4(ga), m_end.to_broadcast([BH, NC, P]), ALU.subtract).then_inc(g_dve, 1)
            V.memset(g2[:, 0:P], 0.0).then_inc(g_dve, 1)
            V.tensor_tensor(c4(g2)[:, 1:NC, :], m_end[:, 0:NC - 1, :].to_broadcast([BH, NC - 1, P]), c4(gm)[:, 1:NC, :],
                            ALU.subtract).then_inc(g_dve, 1)
            V.tensor_tensor(g3[:, :], cs[:, :], gm[:, :], ALU.add).then_inc(g_dve, 1)
            V.memset(gd[:, 0:1], 0.0).then_inc(g_dve, 1)
            me = c4(gm)[:, :, P - 1]
            V.tensor_tensor(gd[:, 1:NC], me[:, 0:NC - 1], me[:, 1:NC], ALU.subtract).then_inc(g_dve, 1)
            V.tensor_copy(ap[0][:, :], ga[:, :]).then_inc(g_dve, 1)
            V.tensor_scalar(mp[0][:, :], gm[:, :], -1.0, None, ALU.mult).then_inc(g_dve, 1)
            dve.wait_ge(g_dve, 13)
            V.tensor_tensor(r1[:, :], ga[:, :], ap[0][:, :], ALU.subtract).then_inc(g_dve, 1)
            V.scalar_tensor_tensor(r2[:, :], gm[:, :], -1.0, mp[0][:, :], ALU.mult, ALU.subtract).then_inc(g_dve, 1)
            dve.wait_ge(g_dve, 15)
            V.tensor_copy(ap[1][:, :], r1[:, :]).then_inc(g_dve, 1)
            V.tensor_copy(mp[1][:, :], r2[:, :]).then_inc(g_dve, 1)
            dve.wait_ge(g_dve, 17)
            V.tensor_tensor(ap[2][:, :], r1[:, :], ap[1][:, :], ALU.subtract).then_inc(g_dve, 1)
            V.tensor_tensor(mp[2][:, :], r2[:, :], mp[1][:, :], ALU.subtract).then_inc(g_dve, 1)

        def g_sync(sp):
            sp.wait_ge(g_dve, 19)
            for k in range(3):
                for q, part in enumerate((ap[k], mp[k])):
                    sp.dma_start(am_d[:, k * NH:(k + 1) * NH, q, :], part[:, :]).then_inc(g_am, 16)

        vv = lambda c: kvb[c][:, D:D + NH * DV]

        def b_sync(sp, b, c):
            t = b * NC + c
            ge(sp, b_hs, t - 3)
            ge(sp, b_ut, b * 3 + (c - 2) if c < 3 else b * 3)
            sp.dma_start(kvb[c][:, :], row(kv, t)).then_inc(b_kv[c], 16)
            sp.dma_start(amb[c][:, :, :], am_d[bass.ds(b, 1), :, :, c * P:(c + 1) * P].rearrange(
                "o k x s -> (o k) x s")).then_inc(b_am[c], 16)
            for j in range(HG):
                rows = slice(DH * j, DH * j + DH)
                sp.dma_start(qbd[c][rows, :, j, :], row(qT_d, t)[rows, :].rearrange("p (g s) -> p g s", g=2)).then_inc(
                    b_q[c], 16)
            sp.dma_start(qtb[c][:, :], row(qT_d, t)).then_inc(b_q[c], 16)

        def w_sync(sp, b, c):
            t = b * NC + c
            w = c % 2
            ge(sp, w_hi, t - 1)
            ge(sp, w_lo, t - 1)
            sp.dma_start(wst[w][:, :], wts[:, bass.ds(t * WCH, WCH)]).then_inc(w_in[w], 16)
            ge(sp, w_lo, t + 1)
            sp.dma_start(whi_d[:, bass.ds(t * WCH, WCH)], wh[w][:, :]).then_inc(w_out[w], 16)
            sp.dma_start(wlo_d[:, bass.ds(t * WCH, WCH)], wl[w][:, :]).then_inc(w_out[w], 16)

        def b_pe(pe, b, c, mid=None):
            t = b * NC + c
            for g in range(2):
                n = t * 2 + g
                ge(pe, b_am[c], b * 16 + 16)
                ge(pe, b_D, n - 1)
                dl = bank[:, g, :]
                nc.tensor.matmul(dl, identb[:, :], maskb[:, :].unsqueeze(1).to_broadcast([P, HG, P]),
                                 start=True, stop=False)
                nc.tensor.matmul(dl, amb[c][:, 0, :],
                                 sel24[:, g * HG:(g + 1) * HG].unsqueeze(2).to_broadcast([24, HG, P]),
                                 start=False, stop=False)
                for j in range(HG):
                    mm = nc.tensor.matmul(bank[:, g, j * P:(j + 1) * P],
                                          sel24[:, g * HG + j:g * HG + j + 1].to_broadcast([24, P]), amb[c][:, 1, :],
                                          start=False, stop=(j == HG - 1))
                mm.then_inc(b_dl, 1)
                ge(pe, b_kv[c], b * 16 + 16)
                ge(pe, b_q[c], b * 80 + 80)
                ge(pe, b_C, n - 1)
                nc.tensor.matmul(bank[:, 2 + g, :], kvb[c][:, g * P:(g + 1) * P],
                                 qbd[c][:, g, :, :].rearrange("p j s -> p (j s)"), start=True, stop=True).then_inc(b_s, 1)
            if mid:
                mid()
            if c < NC - 1:
                ge(pe, b_kw, b * 3 + (c + 1))
                ge(pe, b_ut, b * 3 + c)
                if c == 0:
                    ge(pe, c_lg, b - 1)
                for g in range(2):
                    mm = nc.tensor.matmul(bank[:, 6, g * HG * DV:(g + 1) * HG * DV], kw[:, g * P:(g + 1) * P],
                                          vv(c)[:, g * HG * DV:(g + 1) * HG * DV], start=True, stop=True)
                mm.then_inc(b_u, 1)
            if c:
                ge(pe, b_st, b * 3 + c)
                ge(pe, b_t1, b * 3 + (c - 1))
                for g in range(2):
                    mm = nc.tensor.matmul(bank[:, 5, g * HG * DV:(g + 1) * HG * DV], qtb[c][:, g * P:(g + 1) * P],
                                          St[:, g, :], start=True, stop=True)
                mm.then_inc(b_hi, 1)
            for g in range(2):
                ge(pe, b_C, t * 2 + (g + 1))
                if g == 0:
                    ge(pe, b_hs, t)
                for j in range(HG):
                    hd = g * HG + j
                    mm = nc.tensor.matmul(bank[:, 4, hd * DV:(hd + 1) * DV], Cm[g][:, j * P:(j + 1) * P],
                                          vv(c)[:, hd * DV:(hd + 1) * DV], start=True, stop=True)
            mm.then_inc(b_h, 1)

        def b_act(act, b, c):
            t = b * NC + c
            for g in range(2):
                n = t * 2 + g
                ge(act, b_dl, n + 1)
                ge(act, b_C, n - 1)
                nc.scalar.activation(Dm[g][:, :], bank[:, g, :], ACT.Exp).then_inc(b_D, 1)
            w = c % 2
            ge(act, w_in[w], b * 32 + (16 * (c // 2) + 16))
            ge(act, w_out[w], b * 64 + 32 * (c // 2))
            nc.scalar.copy(wh[w][:, :], wst[w][:, :]).then_inc(w_hi, 1)

        def b_pool(pool, b, c):
            t = b * NC + c
            ge(pool, b_ho, t - 3)
            nc.gpsimd.tensor_copy(colb[c][:, :], col[:, bass.ds(t, 1), :].rearrange("p o k -> p (o k)")).then_inc(b_col, 1)
            if c < NC - 1:
                ge(pool, b_col, t + 1)
                ge(pool, b_kv[c], b * 16 + 16)
                ge(pool, b_u, b * 3 + c)
                vk = vv(c).rearrange("p (h e) -> p h e", e=DV)[:, :, 0:DH]
                nc.gpsimd.tensor_tensor(kw[:, :].rearrange("p (h e) -> p h e", e=DH), vk,
                                        colb[c][:, 0:NH].unsqueeze(2).to_broadcast([P, NH, DH]), ALU.mult).then_inc(b_kw, 1)
            w = c % 2
            ge(pool, w_hi, t + 1)
            ge(pool, w_out[w], b * 64 + 32 * (c // 2))
            nc.gpsimd.tensor_tensor(wl[w][:, :], wst[w][:, :], wh[w][:, :], ALU.subtract).then_inc(w_lo, 1)

        def b_dve(dve, b, c, mid=None):
            V = nc.vector
            t = b * NC + c
            for g in range(2):
                n = t * 2 + g
                ge(dve, b_D, n + 1)
                ge(dve, b_s, n + 1)
                if g == 0:
                    ge(dve, b_h, t)
                V.scalar_tensor_tensor(Cm[g][:, :], bank[:, 2 + g, :], SCALE, Dm[g][:, :], ALU.mult,
                                       ALU.mult).then_inc(b_C, 1)
            if mid:
                mid(0)
            ge(dve, b_col, t + 1)
            if c < NC - 1:
                ge(dve, b_u, b * 3 + (c + 1))
                if c:
                    for g in range(2):
                        V.tensor_scalar(Sd[:, g, :], St[:, g, :], colb[c][:, 3 * NH + g:3 * NH + g + 1], None,
                                        ALU.mult).then_inc(b_sd, 1)
                ub = bank[:, 6, 0:2 * HG * DV].rearrange("p (g e) -> p g e", g=2)
                V.scalar_tensor_tensor(Ut[:, :, :], ub, SCALE, blkm[:, :].unsqueeze(1).to_broadcast([P, 2, HG * DV]),
                                       ALU.mult, ALU.mult).then_inc(b_ut, 1)
                ge(dve, b_ut, b * 3 + (c + 1))
                if c:
                    ge(dve, b_sd, b * 4 + 2 * c)
                    ge(dve, b_hi, b * 3 + c)
                    V.tensor_tensor(St[:, :, :], Sd[:, :, :], Ut[:, :, :], ALU.add).then_inc(b_st, 1)
                else:
                    ge(dve, b_hi, b * 3)
                    V.tensor_copy(St[:, :, :], Ut[:, :, :]).then_inc(b_st, 1)
            if c:
                ge(dve, b_hi, b * 3 + c)
                V.tensor_tensor(t1[:, :, :], bank[:, 5, 0:NH * DV].rearrange("p (h e) -> p h e", e=DV),
                                colb[c][:, NH:2 * NH].unsqueeze(2).to_broadcast([P, NH, DV]), ALU.mult).then_inc(b_t1, 1)
                ge(dve, b_t1, b * 3 + c)
            ge(dve, b_h, t + 1)
            hp = bank[:, 4, 0:NH * DV].rearrange("p (h e) -> p h e", e=DV)
            if c:
                V.tensor_tensor(Hs[:, :, :], hp, t1[:, :, :], ALU.add).then_inc(b_hs, 1)
            else:
                V.tensor_copy(Hs[:, :, :], hp).then_inc(b_hs, 1)
            ge(dve, b_hs, t + 1)
            V.scalar_tensor_tensor(n1[:, :], Hs[:, :, DH], -1.0, Hs[:, :, DH], ALU.mult, ALU.max).then_inc(b_n, 1)
            ge(dve, b_n, t * 3 + 1)
            V.scalar_tensor_tensor(n2[:, :], n1[:, :], N_EPS, colb[c][:, 2 * NH:3 * NH], ALU.add, ALU.max).then_inc(b_n, 1)
            ge(dve, b_n, t * 3 + 2)
            V.reciprocal(n3[:, :], n2[:, :]).then_inc(b_n, 1)
            if mid:
                mid(1)
            ge(dve, b_n, t * 3 + 3)
            if c == 0:
                ge(dve, c_hn, b * 4)
            V.tensor_tensor(h[:, c, :].rearrange("p (h e) -> p h e", e=DH), Hs[:, :, 0:DH],
                            n3[:, :].unsqueeze(2).to_broadcast([P, NH, DH]), ALU.mult).then_inc(b_ho, 1)

        def c_sync(sp, b):
            ge(sp, c_x2, b)
            sp.dma_start(xc[:, :, :], xb_v[bass.ds(b, 1)].rearrange("o p c d -> (o p) c d")).then_inc(c_x, 16)

        def c_dve(dve, b, c, where):
            V = nc.vector
            if c == 0 and where == 0:
                ge(dve, b_ho, b * 4 + 4)
                for k in range(NC):
                    V.bn_stats(st2[:, k, :], h[:, k, :]).then_inc(c_st2, 1)
                ge(dve, c_st2, b * 4 + 4)
                fence(dve)
                for k in range(NC):
                    V.bn_aggr(mv2[:, k, :], st2[:, k, :]).then_inc(c_mv2, 1)
            if c == 0 and where == 1:
                ge(dve, c_rs2, b + 1)
                ge(dve, c_hl, b)
                for k in range(NC):
                    V.tensor_scalar(hn[:, k, :], h[:, k, :], mv2[:, k, 0:1], rs2[:, k:k + 1], ALU.subtract,
                                    ALU.mult).then_inc(c_hn, 1)
            if c == 2 and where == 0:
                ge(dve, c_x2, b + 1)
                for k in range(NC):
                    V.bn_stats(st3[:, k, :], x2[:, k, :]).then_inc(c_st3, 1)
                ge(dve, c_st3, b * 4 + 4)
                fence(dve)
                for k in range(NC):
                    V.bn_aggr(mv3[:, k, :], st3[:, k, :]).then_inc(c_mv3, 1)
            if c == 2 and where == 1:
                ge(dve, c_rs3, b + 1)
                ge(dve, c_yo, b * 16)
                ge(dve, c_yT, b * 2)
                for k in range(NC):
                    V.tensor_scalar(y[:, k, :], x2[:, k, :], mv3[:, k, 0:1], rs3[:, k:k + 1], ALU.subtract,
                                    ALU.mult).then_inc(c_y, 1)

        def c_act(act, b, c):
            if c == 0:
                ge(act, c_mv2, b * 4 + 4)
                nc.scalar.activation(lv2[:, :], mv2[:, :, 1], ACT.Ln, bias=eps_c[:, 0:1]).then_inc(c_lv2, 1)
                ge(act, c_lv2, b + 1)
                nc.scalar.activation(rs2[:, :], lv2[:, :], ACT.Exp, scale=-0.5).then_inc(c_rs2, 1)
            if c == 2:
                ge(act, c_mv3, b * 4 + 4)
                nc.scalar.activation(lv3[:, :], mv3[:, :, 1], ACT.Ln, bias=eps_c[:, 0:1]).then_inc(c_lv3, 1)
                ge(act, c_lv3, b + 1)
                nc.scalar.activation(rs3[:, :], lv3[:, :], ACT.Exp, scale=-0.5).then_inc(c_rs3, 1)
            if c == 3:
                act.dma_start(ov[bass.ds(b, 1)].rearrange("o p c d -> (o p) c d"), x2[:, :, :]).then_inc(c_x2o, 16)
                ge(act, c_y, b * 4 + 4)
                act.dma_start(yv[bass.ds(b, 1), :, :, 0:D].rearrange("o p c d -> (o p) c d"), y[:, :, :]).then_inc(c_yo, 16)
                for k in range(2):
                    ge(act, c_yT, b * 2 + (k + 1))
                    if k == 0:
                        ge(act, c_lp, b)
                    nc.scalar.copy(yT[:, 2 * k:2 * k + 2, :, :].rearrange("p c k t -> p (c k t)"),
                                   bank[:, 7, :]).then_inc(c_yc, 1)
                ge(act, c_lp, b + 1)
                nc.scalar.copy(lg[:, bass.ds(b * 4, 4), :].rearrange("p c e -> p (c e)"),
                               bank[:, 6, 272:272 + NC * NE]).then_inc(c_lg, 1)

        def c_pool(pool, b, c):
            if c == 1:
                ge(pool, c_hn, b * 4 + 4)
                ge(pool, c_x, b * 16 + 16)
                nc.gpsimd.tensor_tensor(hl[:, :, :], hn[:, :, :], lsg[:, :].unsqueeze(1).to_broadcast([P, NC, D]),
                                        ALU.mult).then_inc(c_hl, 1)
                ge(pool, c_hl, b + 1)
                ge(pool, c_y, b * 4)
                ge(pool, c_x2o, b * 16)
                nc.gpsimd.tensor_tensor(x2[:, :, :], hl[:, :, :], xc[:, :, :], ALU.add).then_inc(c_x2, 1)

        def c_pe(pe, b, c):
            if c == 3:
                for k in range(2):
                    ge(pe, c_y, b * 4 + (2 * k + 2))
                    ge(pe, c_yc, b * 2 + k)
                    for j in range(4):
                        mm = nc.tensor.transpose(bank[:, 7, j * P:(j + 1) * P],
                                                 y[:, 2 * k + j // 2, (j % 2) * P:(j % 2 + 1) * P], identf[:, :])
                    mm.then_inc(c_yT, 1)

        def c_pe2(pe, b):
            ge(pe, c_yc, b * 2 + 2)
            ge(pe, c_lg, b)
            for k in range(NC):
                for j in range(KD):
                    mm = nc.tensor.matmul(bank[:, 6, 272 + k * NE:272 + (k + 1) * NE], yT[:, k, j, :], wr[:, j, :],
                                          start=(j == 0), stop=(j == KD - 1))
            mm.then_inc(c_lp, 1)

        V_ = sb("topv", [P, NT, 8]); I_ = sb("topi", [P, NT, 8], U32)
        zr = sb("zr", [P, NT, NE]); er = sb("er", [P, NT, NE]); sc = sb("sc", [P, NT, NE]); sr = sb("sr", [P, NT, NE])
        den = sb("den", [P, NT]); rd = sb("rd", [P, NT]); ck = sb("ck", [P, 2, NT]); ik = sb("ik", [P, 2, NT])
        Mk = sb("Mk", [P, 2, NE, NT]); Mb = sb("Mb", [P, NE, NT], BF16)
        cwm = sb("cwm", [P, 2, NT, NE]); cw16 = sb("cw16", [P, NT, 16])
        tot = sb("tot", [P, NE, NT]); Ci = sb("Ci", [P, NE, NT]); Cx = sb("Cx", [P, NE, NT]); pos = sb("pos", [P, NE, NT])
        pos2 = sb("pos2", [P, NE, NT]); pos3 = sb("pos3", [P, NE, NT])
        ne_ = sb("ne_", [P, NE]); nei = sb("nei", [P, NE], I32); nsi = sb("nsi", [P, NE], I32); nsl = sb("nsl", [P, NE])
        SBi = sb("SBi", [P, NE]); SBx = sb("SBx", [P, NE]); off = sb("off", [P, NE])
        pk = sb("pk", [P, 2, NE, NT]); pk1 = sb("pk1", [P, 2, NT]); pki = sb("pki", [P, 2, NT], I32)
        qki = sb("qki", [P, 2, NT], I32); qk = sb("qk", [P, 2, NT]); rk = sb("rk", [P, 2, NT])
        sle = sb("sle", [P, SLOTS, NE]); esl = sb("esl", [P, SLOTS]); eoff = sb("eoff", [1, SLOTS], I32)
        esm = sb("esm", [P, SLOTS])
        R_ = [sb(f"R{k}", [P, P]) for k in range(4)]; Q_ = [sb(f"Q{k}", [P, NQ]) for k in range(4)]
        TAB = sb("TAB", [P, SLOTS, 4 + NE]); tA = sb("tA", [P, NQ]); tB = sb("tB", [P, NQ])
        r_ch = sem("r_ch"); r_act = sem("r_act"); r_mb = sem("r_mb"); r_rk = sem("r_rk"); r_cw = sem("r_cw")
        r_cwo = sem("r_cwo"); r_eoff = sem("r_eoff"); r_R = sem("r_R"); r_Q = sem("r_Q"); r_mm = sem("r_mm")
        r_tab = sem("r_tab")

        def r_dve(dve):
            V = nc.vector
            n = [0]

            def step(ins):
                n[0] += 1
                ins.then_inc(r_ch, 1)
                dve.wait_ge(r_ch, n[0])

            dve.wait_ge(c_lg, NB)
            V.tensor_tensor(zr[:, :, :], lg[:, :, :], rb[:, :].unsqueeze(1).to_broadcast([P, NT, NE]), ALU.add).then_inc(r_act, 1)
            dve.wait_ge(r_act, 2)
            step(V.tensor_scalar(sr[:, :, :], er[:, :, :], 1.0, None, ALU.add))
            step(V.reciprocal(sc[:, :, :], sr[:, :, :]))
            for t in range(NT):
                ins = V.max(V_[:, t, :], sc[:, t, :])
            step(ins)
            for t in range(NT):
                ins = V.max_index(I_[:, t, :], V_[:, t, :], sc[:, t, :])
            step(ins)
            v12 = V_[:, :, 0:2].rearrange("p t k -> p k t")
            step(V.tensor_copy(ik[:, :, :], I_[:, :, 0:2].rearrange("p t k -> p k t")))
            step(V.scalar_tensor_tensor(den[:, :], V_[:, :, 0], TOP_EPS, V_[:, :, 1], ALU.add, ALU.add))
            step(V.reciprocal(rd[:, :], den[:, :]))
            step(V.scalar_tensor_tensor(ck[:, :, :], v12, tg[:, 1:2], rd[:, :].unsqueeze(1).to_broadcast([P, 2, NT]),
                                        ALU.mult, ALU.mult))
            e_of = rowj[:, 0:NE].unsqueeze(2).to_broadcast([P, NE, NT])
            for k in range(2):
                step(V.tensor_tensor(Mk[:, k, :, :], ik[:, k, :].unsqueeze(1).to_broadcast([P, NE, NT]), e_of, ALU.is_equal))
            V.tensor_tensor(Mb[:, :, :], Mk[:, 0, :, :], Mk[:, 1, :, :], ALU.add).then_inc(r_mb, 1)
            for k in range(2):
                step(V.tensor_tensor(cwm[:, k, :, :], Mk[:, k, :, :].rearrange("p e t -> p t e"),
                                     ck[:, k, :].unsqueeze(2).to_broadcast([P, NT, NE]), ALU.mult))
            V.memset(cw16[:, :, NE:16], 0.0).then_inc(r_cw, 1)
            V.tensor_tensor(cw16[:, :, 0:NE], cwm[:, 0, :, :], cwm[:, 1, :, :], ALU.add).then_inc(r_cw, 1)
            dve.wait_ge(r_rk, 2)
            totp = bank[:, 1, 0:NE * NT]
            step(V.tensor_copy(tot[:, :, :].rearrange("p e t -> p (e t)"), totp))
            step(V.tensor_tensor_scan(Ci[:, :, :].rearrange("p e t -> p (e t)"), ones_row[:, 0:NE * NT],
                                      tot[:, :, :].rearrange("p e t -> p (e t)"), 0.0, ALU.mult, ALU.add))
            step(V.tensor_tensor(Cx[:, :, :], Ci[:, :, :], tot[:, :, :], ALU.subtract))
            step(V.tensor_tensor(ne_[:, :], Ci[:, :, NT - 1], Cx[:, :, 0], ALU.subtract))
            step(V.tensor_scalar(nei[:, :], ne_[:, :], float(SLOT - 1), None, ALU.add))
            step(V.tensor_scalar(nsi[:, :], nei[:, :], 8, None, ALU.arith_shift_right))
            step(V.tensor_copy(nsl[:, :], nsi[:, :]))
            step(V.tensor_tensor_scan(SBi[:, :], ones_row[:, 0:NE], nsl[:, :], 0.0, ALU.mult, ALU.add))
            step(V.tensor_tensor(SBx[:, :], SBi[:, :], nsl[:, :], ALU.subtract))
            step(V.scalar_tensor_tensor(off[:, :], SBx[:, :], float(SLOT), Cx[:, :, 0], ALU.mult, ALU.subtract))
            step(V.tensor_tensor(pos[:, :, :].rearrange("p e t -> p (e t)"), bank[:, 0, 0:NE * NT],
                                 Cx[:, :, :].rearrange("p e t -> p (e t)"), ALU.add))
            step(V.tensor_tensor(pos2[:, :, :], pos[:, :, :], off[:, :].unsqueeze(2).to_broadcast([P, NE, NT]), ALU.add))
            for k in range(2):
                step(V.tensor_tensor(pk[:, k, :, :], Mk[:, k, :, :], pos2[:, :, :], ALU.mult))
                step(V.tensor_reduce(pk1[:, k, :], pk[:, k, :, :].rearrange("p e t -> p t e"), AX.X, ALU.add))
            step(V.tensor_copy(pki[:, :, :], pk1[:, :, :]))
            step(V.tensor_scalar(qki[:, :, :], pki[:, :, :], 7, None, ALU.arith_shift_right))
            step(V.tensor_copy(qk[:, :, :], qki[:, :, :]))
            step(V.scalar_tensor_tensor(rk[:, :, :], qk[:, :, :], -float(P), pk1[:, :, :], ALU.mult, ALU.add))
            step(V.tensor_tensor(sle[:, :, :], SBi[:, :].unsqueeze(1).to_broadcast([P, SLOTS, NE]),
                                 rowj[:, 0:SLOTS].unsqueeze(2).to_broadcast([P, SLOTS, NE]), ALU.is_le))
            step(V.tensor_reduce(esl[:, :], sle[:, :, :], AX.X, ALU.add))
            step(V.tensor_scalar(esm[:, :], esl[:, :], float(NE - 1), None, ALU.min))
            V.tensor_scalar(eoff[:, :], esm[0:1, :], float(WE), None, ALU.mult).then_inc(r_eoff, 1)
            V.tensor_tensor(TAB[:, :, 4:4 + NE], esm[:, :].unsqueeze(2).to_broadcast([P, SLOTS, NE]),
                            rowj[:, 0:NE].unsqueeze(1).to_broadcast([P, SLOTS, NE]), ALU.is_equal).then_inc(r_tab, 1)

        def r_onehot_dve(dve, i):
            V = nc.vector
            for u in range(4):
                t, k = i * 2 + u // 2, u % 2
                ge(dve, r_mm, i * 4 + (u - 3))
                V.tensor_scalar(R_[u][:, :], rowj[:, :], rk[:, k, bass.ds(t, 1)], None, ALU.is_equal).then_inc(r_R, 1)
                V.tensor_scalar(Q_[u][:, :], rowj[:, 0:NQ], qk[:, k, bass.ds(t, 1)], tokp1[:, bass.ds(t, 1)],
                                ALU.is_equal, ALU.mult).then_inc(r_Q, 1)

        def r_onehot_pe(pe, i, first=False, last=False):
            for u in range(4):
                ge(pe, r_R, i * 4 + (u + 1))
                ge(pe, r_Q, i * 4 + (u + 1))
                nc.tensor.matmul(bank[:, 2, 0:NQ], R_[u][:, :], Q_[u][:, :], start=(first and u == 0),
                                 stop=(last and u == 3)).then_inc(r_mm, 1)

        def r_tab_dve(dve):
            V = nc.vector
            dve.wait_ge(r_mm, 2 * NT)
            T1 = bank[:, 2, 0:NQ]
            V.tensor_scalar(tA[:, :], T1, 0.0, SKIP, ALU.is_equal, ALU.mult).then_inc(r_tab, 1)
            V.tensor_scalar(TAB[:, :, 0:2], T1.rearrange("p (s j) -> p s j", j=2), -1.0, 0.0, ALU.add,
                            ALU.max).then_inc(r_tab, 1)
            dve.wait_ge(r_tab, 3)
            V.scalar_tensor_tensor(TAB[:, :, 2:4], T1.rearrange("p (s j) -> p s j", j=2), -1.0,
                                   tA[:, :].rearrange("p (s j) -> p s j", j=2), ALU.add, ALU.add).then_inc(r_tab, 1)

        wfh = [sb(f"wfh{w}", [P, WE], BF16) for w in range(2)]
        wfl = [sb(f"wfl{w}", [P, WE], BF16) for w in range(2)]
        gid = [sb(f"gid{w}", [P, 2], I32) for w in range(2)]
        sid = [sb(f"sid{w}", [P, 2], I32) for w in range(2)]
        xg = [sb(f"xg{w}", [P, 2, YW]) for w in range(2)]
        xh = [sb(f"xh{w}", [P, KD, SLOT], BF16) for w in range(2)]
        xl = [sb(f"xl{w}", [P, KD, SLOT], BF16) for w in range(2)]
        hh = [sb(f"hh{w}", [P, NM, SLOT], BF16) for w in range(2)]
        hl_ = [sb(f"hlo{w}", [P, NM, SLOT], BF16) for w in range(2)]
        sg = [sb(f"sg{w}", [P, SLOT]) for w in range(2)]
        hf = [sb(f"hf{w}", [P, SLOT]) for w in range(3)]
        cwt = [sb(f"cwt{w}", [P, 2, NE]) for w in range(2)]
        cws = [sb(f"cws{w}", [P, 2]) for w in range(2)]
        res = [sb(f"res{w}", [P, 2, D]) for w in range(2)]
        f_w = [sem(f"f_w{w}") for w in range(2)]; f_gid = sem("f_gid"); f_xg = [sem(f"f_xg{w}") for w in range(2)]
        f_T = sem("f_T"); f_xh = sem("f_xh"); f_xl = sem("f_xl"); f_l1 = sem("f_l1"); f_sg = sem("f_sg")
        f_hf = sem("f_hf"); f_hh = sem("f_hh"); f_hl = sem("f_hl"); f_y = sem("f_y"); f_cwt = sem("f_cwt")
        f_cws = sem("f_cws"); f_res = sem("f_res"); f_sid = sem("f_sid"); f_out = sem("f_out")

        def f_sync(sp, s, w):
            e = sp.value_load(eoff[0:1, bass.ds(s, 1)], min_val=0, max_val=(NE - 1) * WE)
            ge(sp, f_y, s - 1)
            sp.dma_start(wfh[w][:, :], whi_d[:, bass.ds(e, WE)]).then_inc(f_w[w], 16)
            sp.dma_start(wfl[w][:, :], wlo_d[:, bass.ds(e, WE)]).then_inc(f_w[w], 16)

        def half(v, w):
            return v // 2 if isinstance(v, int) else None

        def f_gather(pool, s, sh, w):
            ge(pool, f_T, s - 1)
            ge(pool, f_cwt, s - 1)
            nc.gpsimd.tensor_copy(gid[w][:, :], TAB[:, bass.ds(s, 1), 0:2].rearrange("p o k -> p (o k)")).then_inc(f_gid, 1)
            ge(pool, f_gid, s + 1)
            for j in range(2):
                nc.gpsimd.indirect_dma_start(xg[w][:, j, :], None, y_d,
                                             bass.IndirectOffsetOnAxis(ap=gid[w][:, j:j + 1], axis=0)).then_inc(f_xg[w], 16)

        def f_scatter(pool, s, w):
            ge(pool, f_out, s * 32)
            nc.gpsimd.tensor_copy(sid[w][:, :], TAB[:, bass.ds(s, 1), 2:4].rearrange("p o k -> p (o k)")).then_inc(f_sid, 1)
            ge(pool, f_sid, s + 1)
            ge(pool, f_res, s * 2 + 2)
            for j in range(2):
                if j:
                    ge(pool, f_out, s * 32 + 16)
                nc.gpsimd.indirect_dma_start(out, bass.IndirectOffsetOnAxis(ap=sid[w][:, j:j + 1], axis=0),
                                             res[w][:, j, :], None, bounds_check=TOK - 1, oob_is_err=False,
                                             compute_op=ALU.add).then_inc(f_out, 16)

        XT = lambda w: bank[:, w, :].rearrange("p (k t) -> p k t", k=KD)

        def f_T_pe(pe, s, sh, w):
            ge(pe, f_xg[w], sh * 32 + 32)
            ge(pe, f_xl, s - 1)
            for j in range(2):
                for k in range(KD):
                    mm = nc.tensor.transpose(XT(w)[:, k, j * P:(j + 1) * P], xg[w][:, j, k * P:(k + 1) * P], identf[:, :])
            mm.then_inc(f_T, 1)

        def three(dst, pairs):
            for n, (l, r) in enumerate(pairs):
                mm = nc.tensor.matmul(dst, l, r, start=(n == 0), stop=(n == len(pairs) - 1))
            return mm

        def f_l1_pe(pe, s, sh, w):
            ge(pe, f_w[w], sh * 32 + 32)
            ge(pe, f_xh, s + 1)
            ge(pe, f_xl, s + 1)
            for m in range(NM):
                n = s * NM + m
                ge(pe, f_hf, n - 3)
                bk = 2 + (NM * w + m) % 4
                for q in range(2 if m < NM - 1 else 1):
                    pairs = []
                    for k in range(KD):
                        c0 = k * 2 * HID + (2 * m + q) * P
                        H_, L_ = wfh[w][:, c0:c0 + P], wfl[w][:, c0:c0 + P]
                        pairs += [(H_, xh[w][:, k, :]), (H_, xl[w][:, k, :]), (L_, xh[w][:, k, :])]
                    mm = three(bank[:, bk, q * SLOT:(q + 1) * SLOT], pairs)
                mm.then_inc(f_l1, 1)

        def f_l2_pe(pe, s, w):
            ge(pe, f_hh, s * NM + NM)
            ge(pe, f_hl, s * NM + NM)
            ge(pe, f_res, s * 2 - 2)
            for j in range(2):
                pairs = []
                for m in range(NM):
                    K = P if m < NM - 1 else HREM
                    c0 = W13 + m * D
                    hi, lo = hh[w][0:K, m, j * P:(j + 1) * P], hl_[w][0:K, m, j * P:(j + 1) * P]
                    pairs += [(hi, wfh[w][0:K, c0:c0 + D]), (hi, wfl[w][0:K, c0:c0 + D]), (lo, wfh[w][0:K, c0:c0 + D])]
                mm = three(bank[:, 6 + w, j * D:(j + 1) * D], pairs)
            mm.then_inc(f_y, 1)

        def f_x_act(act, s, w):
            ge(act, f_T, s + 1)
            ge(act, f_l1, s * NM - NM)
            nc.scalar.copy(xh[w][:, :, :], XT(w)).then_inc(f_xh, 1)

        def f_x_dve(dve, s, sh, w):
            V = nc.vector
            ge(dve, f_xg[w], sh * 32 + 32)
            ge(dve, f_cws, s - 1)
            V.tensor_tensor(cwt[w][:, :, :], xg[w][:, :, D:D + NE],
                            TAB[:, bass.ds(s, 1), 4:4 + NE].to_broadcast([P, 2, NE]), ALU.mult).then_inc(f_cwt, 1)
            ge(dve, f_xh, s + 1)
            ge(dve, f_l1, s * NM - NM)
            V.tensor_tensor(xl[w][:, :, :], XT(w), xh[w][:, :, :], ALU.subtract).then_inc(f_xl, 1)

        def f_h_act(act, s, w):
            def hi(m):
                K = P if m < NM - 1 else HREM
                n = s * NM + m
                ge(act, f_hf, n + 1)
                if m == 0:
                    ge(act, f_y, s - 1)
                nc.scalar.copy(hh[w][0:K, m, :], hf[m % 3][0:K, :]).then_inc(f_hh, 1)
            for m in range(NM):
                K = P if m < NM - 1 else HREM
                n = s * NM + m
                ge(act, f_l1, n + 1)
                ge(act, f_hf, n - 1)
                nc.scalar.activation(sg[m % 2][0:K, :], bank[0:K, 2 + (NM * w + m) % 4, 0:SLOT], ACT.Silu).then_inc(f_sg, 1)
                if m:
                    hi(m - 1)
            hi(NM - 1)

        def f_h_dve(dve, s, w):
            V = nc.vector

            def lo(m):
                K = P if m < NM - 1 else HREM
                n = s * NM + m
                ge(dve, f_hh, n + 1)
                if m == 0:
                    ge(dve, f_y, s - 1)
                V.tensor_tensor(hl_[w][0:K, m, :], hf[m % 3][0:K, :], hh[w][0:K, m, :], ALU.subtract).then_inc(f_hl, 1)
            ge(dve, f_cwt, s + 1)
            ge(dve, f_res, s * 2 - 2)
            V.tensor_reduce(cws[w][:, :], cwt[w][:, :, :], AX.X, ALU.add).then_inc(f_cws, 1)
            for m in range(NM):
                n = s * NM + m
                ge(dve, f_sg, n + 1)
                ge(dve, f_hl, n - 2)
                ge(dve, f_hh, n - 2)
                bk = 2 + (NM * w + m) % 4
                if m < NM - 1:
                    V.tensor_tensor(hf[m % 3][:, :], sg[m % 2][:, :], bank[:, bk, SLOT:2 * SLOT], ALU.mult).then_inc(f_hf, 1)
                else:
                    V.tensor_tensor(hf[m % 3][0:HREM, :], sg[m % 2][0:HREM, :], bank[HREM:P, bk, 0:SLOT],
                                    ALU.mult).then_inc(f_hf, 1)
                if m:
                    lo(m - 1)
            lo(NM - 1)

        def f_e_dve(dve, s, w):
            ge(dve, f_y, s + 1)
            ge(dve, f_cws, s + 1)
            ge(dve, f_out, s * 32 - 32)
            for j in range(2):
                nc.vector.tensor_scalar(res[w][:, j, :], bank[:, 6 + w, j * D:(j + 1) * D], cws[w][:, j:j + 1], None,
                                        ALU.mult).then_inc(f_res, 1)

        def f_pe(pe, s, sh, w, t_next=True, prev=True):
            f_l1_pe(pe, s, sh, w)
            if t_next:
                f_T_pe(pe, s + 1, sh + w, 1 - w)
            if prev:
                f_l2_pe(pe, s - 1, 1 - w)

        def f_act(act, s, sh, w, t_next=True, prev=True):
            f_h_act(act, s, w)
            if t_next:
                f_x_act(act, s + 1, 1 - w)

        def f_dve(dve, s, sh, w, t_next=True, prev=True):
            f_h_dve(dve, s, w)
            if t_next:
                f_x_dve(dve, s + 1, sh + w, 1 - w)
            if prev:
                f_e_dve(dve, s - 1, 1 - w)

        def slots(eng, step):
            step(eng, 0, 0, 0, True, False)
            for s in range(1, 4):
                step(eng, s, s // 2, s % 2)
            with eng.Fori(2, SLOTS // 2 - 1) as i:
                for w in range(2):
                    step(eng, i * 2 + w, i, w)
            step(eng, SLOTS - 2, SLOTS // 2 - 1, 0)
            step(eng, SLOTS - 1, SLOTS // 2 - 1, 1, False, True)

        block = ctx.enter_context(nc.Block())

        @block.sync
        def _(sp):
            sp.dma_start(wg[:, :, :], wgate).then_inc(s_small, 16)
            sp.dma_start(ifb_s[:, :], ifb).then_inc(s_small, 16)
            sp.dma_start(lnr[:, :], lnrow).then_inc(s_small, 16)
            sp.dma_start(gs[:, :], gsc).then_inc(s_small, 16)
            sp.dma_start(wr[:, :, :], wroute).then_inc(s_small, 16)
            sp.dma_start(rb[:, :], rbias).then_inc(s_small, 16)
            a_sync(sp, 0)
            with sp.Fori(1, NT // 8) as i:
                a_sync(sp, i)
            g_sync(sp)
            sp.wait_ge(s_qz, NC)
            sp.wait_ge(g_am, 16 * 6)
            for u in range(8):
                sp.wait_ge(a_qo[u], 16 * NT // 8)
            for c in range(NC):
                b_sync(sp, 0, c)
                w_sync(sp, 0, c)

            def batch(b):
                for c in range(NC):
                    b_sync(sp, b, c)
                    if c == 0:
                        c_sync(sp, b - 1)
                    w_sync(sp, b, c)

            batch(1)
            with sp.Fori(2, NB) as b:
                batch(b)
            c_sync(sp, NB - 1)
            for w in range(2):
                sp.wait_ge(w_out[w], 32 * NT // 2)
            sp.wait_ge(r_eoff, 1)
            f_sync(sp, 0, 0)
            f_sync(sp, 1, 1)
            with sp.Fori(1, SLOTS // 2) as i:
                for w in range(2):
                    f_sync(sp, i * 2 + w, w)

        @block.scalar
        def _(act):
            consts_act(act)
            act.wait_ge(s_const, NCONST)
            a_act(act, 0)
            with act.Fori(1, NT // 8) as i:
                a_act(act, i)
            g_actf_all(act)
            for c in range(NC):
                b_act(act, 0, c)

            def batch(b):
                for c in range(NC):
                    b_act(act, b, c)
                    c_act(act, b - 1, c)

            batch(1)
            with act.Fori(2, NB) as b:
                batch(b)
            for c in range(NC):
                c_act(act, NB - 1, c)
            act.wait_ge(r_act, 1)
            nc.scalar.activation(er[:, :, :], zr[:, :, :], ACT.Exp, scale=-1.0).then_inc(r_act, 1)
            act.wait_ge(r_cw, 2)
            act.wait_ge(c_yo, 16 * NB)
            act.dma_start(y_d[:, D:YW].rearrange("(t p) e -> p t e", p=P), cw16[:, :, :]).then_inc(r_cwo, 16)
            f_x_act(act, 0, 0)
            slots(act, f_act)

        @block.vector
        def _(dve):
            consts_dve(dve)
            a_dve(dve, 0)
            with dve.Fori(1, NT // 8) as i:
                a_dve(dve, i)
            g_dvef(dve)
            for c in range(NC):
                b_dve(dve, 0, c)

            def batch(b):
                for c in range(NC):
                    b_dve(dve, b, c, mid=lambda where: c_dve(dve, b - 1, c, where))

            batch(1)
            with dve.Fori(2, NB) as b:
                batch(b)
            for c in range(NC):
                for where in range(2):
                    c_dve(dve, NB - 1, c, where)
            r_dve(dve)
            r_onehot_dve(dve, 0)
            with dve.Fori(1, NT // 2) as i:
                r_onehot_dve(dve, i)
            r_tab_dve(dve)
            f_x_dve(dve, 0, 0, 0)
            slots(dve, f_dve)
            f_e_dve(dve, SLOTS - 1, 1)

        @block.gpsimd
        def _(pool):
            consts_pool(pool)
            pool.wait_ge(s_lsg, 1)
            pool.wait_ge(g_cols, 4)
            for c in range(NC):
                b_pool(pool, 0, c)

            def batch(b):
                for c in range(NC):
                    b_pool(pool, b, c)
                    c_pool(pool, b - 1, c)

            batch(1)
            with pool.Fori(2, NB) as b:
                batch(b)
            c_pool(pool, NB - 1, 1)
            pool.wait_ge(r_tab, 4)
            pool.wait_ge(r_cwo, 16)
            pool.wait_ge(c_x2o, 16 * NB)
            f_gather(pool, 0, 0, 0)
            f_gather(pool, 1, 0, 1)
            f_gather(pool, 2, 1, 0)

            def rows_in_out(i):
                f_gather(pool, i * 2 + 1, i, 1)
                f_scatter(pool, i * 2 - 2, 0)
                f_gather(pool, i * 2 + 2, i + 1, 0)
                f_scatter(pool, i * 2 - 1, 1)

            rows_in_out(1)
            with pool.Fori(2, SLOTS // 2 - 1) as i:
                rows_in_out(i)
            f_gather(pool, SLOTS - 1, SLOTS // 2 - 1, 1)
            for s in range(SLOTS - 4, SLOTS):
                f_scatter(pool, s, s % 2)
            pool.wait_ge(f_out, 32 * SLOTS)

        @block.tensor
        def _(pe):
            pe.wait_ge(s_const, NCONST)
            pe.wait_ge(s_wgkv, 1)
            a_pe(pe, 0)
            with pe.Fori(1, NT // 8) as i:
                a_pe(pe, i)
            g_pe_all(pe)
            for c in range(NC):
                b_pe(pe, 0, c)

            def batch(b):
                for c in range(NC):
                    b_pe(pe, b, c, mid=lambda: c_pe(pe, b - 1, c))
                    if c == 3:
                        c_pe2(pe, b - 1)

            batch(1)
            with pe.Fori(2, NB) as b:
                batch(b)
            c_pe(pe, NB - 1, 3)
            c_pe2(pe, NB - 1)
            pe.wait_ge(r_mb, 1)
            mb = Mb[:, :, :].rearrange("p e t -> p (e t)")
            nc.tensor.matmul(bank[:, 0, 0:NE * NT], upperb[:, :], mb, start=True, stop=True).then_inc(r_rk, 1)
            nc.tensor.matmul(bank[:, 1, 0:NE * NT], onesb[:, :], mb, start=True, stop=True).then_inc(r_rk, 1)
            r_onehot_pe(pe, 0, first=True)
            with pe.Fori(1, NT // 2 - 1) as i:
                r_onehot_pe(pe, i)
            r_onehot_pe(pe, NT // 2 - 1, last=True)
            f_T_pe(pe, 0, 0, 0)
            slots(pe, f_pe)
            f_l2_pe(pe, SLOTS - 1, 1)



_IN = ['x', 'kv', 'wgate', 'ifb', 'lnrow', 'gsc', 'wroute', 'rbias', 'wts']


def layout(i):
    import numpy as np
    a = {k: np.asarray(v) for k, v in i.items()}
    x = a['x'].reshape(TOK, D)
    ctx = a['ctx_1024'].reshape(NT, P, D)
    kT = ctx.transpose(0, 2, 1).reshape(NT, KD, P, P).transpose(0, 2, 1, 3).reshape(NT, P, D)
    v = np.concatenate([ctx.reshape(NT, P, NH, DH), np.ones((NT, P, NH, 1), np.float32)], -1).reshape(NT, P, NH * DV)
    kv = np.concatenate([kT, v], -1)
    gw = np.concatenate([a['L0_xattn_igate_w'], a['L0_xattn_fgate_w']], 0).T
    wgate = gw.reshape(6, P, 2 * NH).transpose(1, 0, 2)
    ifb = np.stack([np.tile(a['L0_xattn_igate_b'], NB), np.tile(a['L0_xattn_fgate_b'], NB)], 1)
    lnrow = np.tile(a['L0_xattn_ln_scale'][None], (P, 1))
    gsc = np.tile(np.stack([a['g_xattn'][0], a['g_ffn'][0]])[None], (P, 1))
    gate = np.concatenate([a['L0_ffn_gate_weight'], a['L0_ffn_new_gate_weight']], 0).T
    wroute = gate.reshape(KD, P, NE).transpose(1, 0, 2)
    rbias = np.tile(np.concatenate([np.zeros(NE - 1, np.float32), a['L0_ffn_gate_bias']])[None], (P, 1))
    cat = lambda n: np.concatenate([a[f'L0_ffn_{n}'], a[f'L0_ffn_new_{n}']], 0)
    w1, w3 = (cat(n).transpose(0, 2, 1) for n in ('w1', 'w3'))
    full = (NM - 1) * P
    m13 = np.stack([w1[:, :, :full].reshape(NE, D, NM - 1, P), w3[:, :, :full].reshape(NE, D, NM - 1, P)], 3)
    w13 = np.concatenate([m13.reshape(NE, D, 2 * full), w1[:, :, full:], w3[:, :, full:]], -1)
    w13 = w13.reshape(NE, KD, P, 2 * HID).transpose(2, 0, 1, 3).reshape(P, NE, W13)
    w2 = cat('w2').transpose(0, 2, 1)
    w2 = np.concatenate([w2, np.zeros((NE, NM * P - HID, D), np.float32)], 1)
    w2 = w2.reshape(NE, NM, P, D).transpose(2, 0, 1, 3).reshape(P, NE, W2C)
    wts = np.concatenate([w13, w2], -1).reshape(P, WALL)
    made = dict(x=x, kv=kv, wgate=wgate, ifb=ifb, lnrow=lnrow, gsc=gsc, wroute=wroute, rbias=rbias, wts=wts)
    return {k: np.ascontiguousarray(v) for k, v in made.items()}


def kernel(**inputs):
    import concourse.bacc as _bacc
    from concourse import mybir as _mybir
    from concourse.bass_utils import run_bass_kernel_spmd as _run

    nc = _bacc.Bacc("TRN2", target_bir_lowering=False, num_devices=1)
    made = layout(inputs)
    arrays, args = {}, []
    for name in _IN:
        v = made[name]
        arrays[f"in_{name}"] = v
        args.append(nc.dram_tensor(f"in_{name}", v.shape, _mybir.dt.from_np(v.dtype), kind="ExternalInput").ap())
    args.append(nc.dram_tensor("out_0", (TOK, D), _mybir.dt.float32, kind="ExternalOutput").ap())
    build(nc, *args)
    r = _run(nc, [arrays], core_ids=[0])
    return r.results[0]["out_0"].reshape(NB, S, D)
```

```python
from contextlib import ExitStack

import concourse.bass as bass
from concourse import mybir

ALU = mybir.AluOpType
ACT = mybir.ActivationFunctionType
AX = mybir.AxisListType
F32 = mybir.dt.float32
BF16 = mybir.dt.bfloat16
I32 = mybir.dt.int32
U32 = mybir.dt.uint32

P = 128
NB, S, D, NH = 8, 512, 256, 8
DH = D // NH
DV = DH + 1
NC = S // P
NT = NB * NC
BH = NB * NH
TOK = NB * S
NE, HID, TOPK = 9, 704, 2
KD = D // P
HG = 4
NM = 6
HREM = HID - 5 * P
W13 = KD * 2 * HID
W2C = NM * D
WE = W13 + W2C
WALL = NE * WE
WCH = WALL // NT
SLOT = 256
SLOTS = (TOK * TOPK + NE * (SLOT - 1)) // SLOT
NQ = SLOTS * SLOT // P
YW = D + 16
SKIP = 8192.0
LN_EPS, N_EPS, TOP_EPS = 1e-5, 1e-6, 1e-20
SCALE = float(1.0 / DH ** 0.5)
NEG = -1e30


def build(nc, x, kv, wgate, ifb, lnrow, gsc, wroute, rbias, wts, out):
    with ExitStack() as ctx:
        def sb(name, shape, dt=F32):
            return ctx.enter_context(nc.sbuf_tensor(name, shape, dt))

        def sem(name):
            return ctx.enter_context(nc.semaphore(name))

        def dram(name, shape, dt):
            return nc.dram_tensor(name, shape, dt, kind="Internal").ap()

        qT_d = dram("qT_d", [NT, P, D], F32)
        am_d = dram("am_d", [NB, 3 * NH, 2, S], BF16)
        w_d = dram("w_d", [P, 2, WALL], BF16)
        y_d = dram("y_d", [TOK, YW], F32)

        bank = ctx.enter_context(nc.psum_tensor("bank", [P, 8, 512], F32))

        rowj = sb("rowj", [P, P]); pcol = sb("pcol", [P, 1]); blk = sb("blk", [P, HG * DV])
        tokp1 = sb("tokp1", [P, NT])
        identf = sb("identf", [P, P]); identb = sb("identb", [P, P], BF16)
        upperb = sb("upperb", [P, P], BF16); onesb = sb("onesb", [P, P], BF16)
        maskb = sb("maskb", [P, P], BF16); sel24 = sb("sel24", [24, NH], BF16)
        selt = sb("selt", [24, NH]); blkm = sb("blkm", [P, HG * DV]); blkt = sb("blkt", [P, HG * DV])
        eps_c = sb("eps_c", [P, 1]); one_c = sb("one_c", [P, 1]); neps = sb("neps", [P, 1])
        ones_row = sb("ones_row", [P, S])
        wg = sb("wg", [P, 6, 2 * NH]); wgkv = sb("wgkv", [P, 2, 2 * NH]); ifb_s = sb("ifb_s", [BH, 2])
        lnr = sb("lnr", [P, D]); gs = sb("gs", [P, 2]); tg = sb("tg", [P, 2]); lsg = sb("lsg", [P, D])
        wr = sb("wr", [P, KD, NE]); rb = sb("rb", [P, NE])

        col = sb("col", [P, NT, 3 * NH + 2])
        kvb = [sb(f"kvb{c}", [P, D + NH * DV]) for c in range(NC)]
        qtb = [sb(f"qtb{c}", [P, D]) for c in range(NC)]
        qbd = [sb(f"qbd{w}", [P, 2, HG, P]) for w in range(2)]
        amb = [sb(f"amb{c}", [24, 2, P], BF16) for c in range(NC)]
        colb = [sb(f"colb{c}", [P, 3 * NH + 2]) for c in range(NC)]
        Dm = [sb(f"Dm{g}", [P, 512]) for g in range(2)]
        Cm = [sb(f"Cm{g}", [P, 512]) for g in range(2)]
        Ch = [sb(f"Ch{k}", [P, 512], BF16) for k in range(4)]
        Cl = [sb(f"Cl{k}", [P, 512], BF16) for k in range(4)]
        vp = [sb(f"vp{w}", [P, NH, 2, DV], BF16) for w in range(2)]
        kw = [sb(f"kw{w}", [P, D]) for w in range(2)]; St = sb("St", [P, 2, HG * DV]); Sd = sb("Sd", [P, 2, HG * DV])
        Ut = sb("Ut", [P, 2, HG * DV])
        t1 = sb("t1", [P, NH, DV]); t2 = sb("t2", [P, NH, DV]); Hs = sb("Hs", [P, NH, DV])
        n1 = sb("n1", [P, NH]); n2 = sb("n2", [P, NH]); n3 = sb("n3", [P, NH])
        h = sb("h", [P, NC, D])
        wst = [sb(f"wst{w}", [P, WCH]) for w in range(2)]
        whl = [sb(f"whl{w}", [P, 2, WCH], BF16) for w in range(2)]
        xc = sb("xc", [P, NC, D]); st2 = sb("st2", [P, NC, 6]); mv2 = sb("mv2", [P, NC, 2])
        lv2 = sb("lv2", [P, NC]); rs2 = sb("rs2", [P, NC]); hn = sb("hn", [P, NC, D]); hl = sb("hl", [P, NC, D])
        x2 = sb("x2", [P, NC, D])
        st3 = sb("st3", [P, NC, 6]); mv3 = sb("mv3", [P, NC, 2]); lv3 = sb("lv3", [P, NC]); rs3 = sb("rs3", [P, NC])
        y = sb("y", [P, NC, D]); yT = sb("yT", [P, NC, KD, P]); lg = sb("lg", [P, NT, NE])

        early_ctx = ExitStack()

        def early(name, shape, dt=F32):
            return early_ctx.enter_context(nc.sbuf_tensor(name, shape, dt))

        xa = [early(f"xa{h}", [P, NC, D]) for h in range(2)]
        ka = [early(f"ka{h}", [P, NC, D]) for h in range(2)]
        stA = early("stA", [P, 8, 6]); mvA = early("mvA", [P, 8, 2]); lvA = early("lvA", [P, 8]); rsA = early("rsA", [P, 8])
        qn = [early(f"qn{u}", [P, D]) for u in range(8)]
        qt = [early(f"qt{h}", [P, NC, D]) for h in range(2)]
        gall = early("gall", [P, NC, 2, NB, NH])
        z = early("z", [BH, S]); g1 = early("g1", [BH, S]); g2 = early("g2", [BH, S]); g3 = early("g3", [BH, S])
        lf = early("lf", [BH, S]); cs = early("cs", [BH, S]); ga = early("ga", [BH, S]); gm = early("gm", [BH, S])
        r1 = early("r1", [BH, S]); r2 = early("r2", [BH, S])
        ap = [early(f"ap{k}", [BH, S], BF16) for k in range(3)]
        mp = [early(f"mp{k}", [BH, S], BF16) for k in range(3)]
        gw = early("gw", [BH, S]); gE = early("gE", [BH, S]); gn = early("gn", [BH, S]); gd = early("gd", [BH, NC])
        gdx = early("gdx", [BH, NC]); spread = early("spread", [BH, BH * DH])
        early_ctx.close()

        s_iota = sem("s_iota"); s_const = sem("s_const"); s_small = sem("s_small"); s_tanh = sem("s_tanh")
        s_qz = sem("s_qz"); s_wgkv = sem("s_wgkv"); s_lsg = sem("s_lsg")
        a_x = [sem(f"a_x{h}") for h in range(2)]; a_k = [sem(f"a_k{h}") for h in range(2)]
        a_st = sem("a_st"); a_mv = sem("a_mv"); a_lv = sem("a_lv"); a_rs = sem("a_rs"); a_q = sem("a_q")
        a_tr = sem("a_tr"); a_qt = sem("a_qt"); a_gp = sem("a_gp"); a_gs = sem("a_gs")
        a_qo = [sem(f"a_qo{h}") for h in range(2)]
        g_spread = sem("g_spread"); g_tp = sem("g_tp"); g_act = sem("g_act"); g_dve = sem("g_dve"); g_am = sem("g_am"); g_col = sem("g_col")
        g_dec = sem("g_dec"); g_cols = sem("g_cols")
        b_kv = [sem(f"b_kv{c}") for c in range(NC)]; b_q = [sem(f"b_q{c}") for c in range(NC)]
        b_am = [sem(f"b_am{c}") for c in range(NC)]; b_col = sem("b_col")
        b_dl = sem("b_dl"); b_s = sem("b_s"); b_D = sem("b_D"); b_C = sem("b_C")
        b_qb = sem("b_qb"); b_kw = sem("b_kw"); b_u = sem("b_u"); b_ut = sem("b_ut"); b_st = sem("b_st"); b_hi = sem("b_hi")
        b_t1 = sem("b_t1"); b_h = sem("b_h"); b_hs = sem("b_hs"); b_n = sem("b_n"); b_ho = sem("b_ho")
        b_sd = sem("b_sd"); b_Ch = sem("b_Ch"); b_Cl = sem("b_Cl"); b_vh = sem("b_vh"); b_vl = sem("b_vl")
        b_t2 = sem("b_t2")
        w_in = [sem(f"w_in{w}") for w in range(2)]; w_hi = sem("w_hi"); w_lo = sem("w_lo")
        w_out = [sem(f"w_out{w}") for w in range(2)]
        c_x = sem("c_x"); c_st2 = sem("c_st2"); c_mv2 = sem("c_mv2"); c_lv2 = sem("c_lv2"); c_rs2 = sem("c_rs2")
        c_hn = sem("c_hn"); c_hl = sem("c_hl"); c_x2 = sem("c_x2"); c_st3 = sem("c_st3"); c_mv3 = sem("c_mv3")
        c_lv3 = sem("c_lv3"); c_rs3 = sem("c_rs3"); c_y = sem("c_y"); c_yT = sem("c_yT"); c_yc = sem("c_yc")
        c_lp = sem("c_lp"); c_lg = sem("c_lg"); c_x2o = sem("c_x2o"); c_yo = sem("c_yo")
        s_pace = sem("s_pace")

        def fence(eng):
            eng.sem_inc(s_pace, 1)

        def ge(eng, sem, val):
            if isinstance(val, int):
                if val > 0:
                    eng.wait_ge(sem, val)
                return
            eng.wait_ge(sem, val)
            if eng.engine in (nc.sync.engine, nc.gpsimd.engine):
                fence(eng)

        x_v = x.rearrange("(t p) d -> p t d", p=P)
        k_v = kv.rearrange("t p k -> p t k")
        qT_v = qT_d.rearrange("t p d -> p t d")
        ov = out.rearrange("(b c p) d -> b p c d", p=P, c=NC)
        x_b = x.rearrange("(b c p) d -> b p c d", p=P, c=NC)
        yv = y_d.rearrange("(b c p) d -> b p c d", p=P, c=NC)

        def row(v, i, n=1):
            return v[bass.ds(i, n)].rearrange("o p d -> (o p) d")

        def consts_pool(pool):
            nc.gpsimd.iota(rowj[:, :], [[1, P]], base=0, channel_multiplier=0,
                           allow_small_or_imprecise_dtypes=True).then_inc(s_iota, 1)
            nc.gpsimd.iota(pcol[:, :], [[1, 1]], base=0, channel_multiplier=1,
                           allow_small_or_imprecise_dtypes=True).then_inc(s_iota, 1)
            nc.gpsimd.iota(blk[:, :].rearrange("p (h e) -> p h e", e=DV), [[DH, HG], [0, DV]], base=0,
                           channel_multiplier=0, allow_small_or_imprecise_dtypes=True).then_inc(s_iota, 1)
            nc.gpsimd.iota(tokp1[:, :], [[P, NT]], base=1, channel_multiplier=1,
                           allow_small_or_imprecise_dtypes=True).then_inc(s_iota, 1)
            for w in range(2):
                nc.gpsimd.memset(qbd[w][:, :, :, :], 0.0).then_inc(s_qz, 1)

        NCONST = 14

        def consts_dve(dve):
            nc.vector.memset(eps_c[:, :], LN_EPS).then_inc(s_const, 1)
            nc.vector.memset(one_c[:, :], 1.0).then_inc(s_const, 1)
            nc.vector.memset(neps[:, :], N_EPS).then_inc(s_const, 1)
            nc.vector.memset(ones_row[:, :], 1.0).then_inc(s_const, 1)
            nc.vector.memset(onesb[:, :], 1.0).then_inc(s_const, 1)
            dve.wait_ge(s_iota, 4)
            nc.vector.tensor_scalar(identf[:, :], rowj[:, :], pcol[:, 0:1], None, ALU.is_equal).then_inc(s_const, 1)
            nc.vector.tensor_scalar(identb[:, :], rowj[:, :], pcol[:, 0:1], None, ALU.is_equal).then_inc(s_const, 1)
            nc.vector.tensor_scalar(upperb[:, :], rowj[:, :], pcol[:, 0:1], None, ALU.is_gt).then_inc(s_const, 1)
            nc.vector.tensor_scalar(maskb[:, :], rowj[:, :], pcol[:, 0:1], NEG, ALU.is_lt, ALU.mult).then_inc(s_const, 1)
            nc.vector.tensor_scalar(blkt[:, :], blk[:, :], float(DH), pcol[:, 0:1], ALU.add, ALU.is_gt).then_inc(s_const, 1)
            nc.vector.tensor_scalar(blkm[:, :], blk[:, :], pcol[:, 0:1], None, ALU.is_le).then_inc(s_const, 1)
            dve.wait_ge(s_const, 11)
            nc.vector.tensor_tensor(blkm[:, :], blkm[:, :], blkt[:, :], ALU.mult).then_inc(s_const, 1)
            nc.vector.tensor_tensor(selt[:, :], identf[0:24, 0:8], identf[0:24, 8:16], ALU.add).then_inc(s_const, 1)
            dve.wait_ge(s_const, 13)
            nc.vector.tensor_tensor(sel24[:, :], selt[:, :], identf[0:24, 16:24], ALU.add).then_inc(s_const, 1)

        def wgkv_dve(dve):
            dve.wait_ge(s_small, 16 * 6)
            nc.vector.tensor_tensor(wgkv[:, :, :], wg[:, 2:4, :], wg[:, 4:6, :], ALU.add).then_inc(s_wgkv, 1)

        def lsg_dve(dve):
            dve.wait_ge(s_tanh, 1)
            nc.vector.tensor_scalar(lsg[:, :], lnr[:, :], tg[:, 0:1], None, ALU.mult).then_inc(s_lsg, 1)

        def consts_act(act):
            act.wait_ge(s_small, 16 * 6)
            nc.scalar.activation(tg[:, :], gs[:, :], ACT.Tanh).then_inc(s_tanh, 1)

        def a_x_sync(sp, i):
            for h in range(2):
                ge(sp, a_q, i * 8 + (h * NC - 4))
                sp.dma_start(xa[h][:, :, :], x_v[:, bass.ds(i * 8 + h * NC, NC), :]).then_inc(a_x[h], 16)

        def a_k_sync(sp, i):
            for h in range(2):
                ge(sp, a_gp, i * 4 + (h * 2 - 2))
                sp.dma_start(ka[h][:, :, :], k_v[:, bass.ds(i * 8 + h * NC, NC), 0:D]).then_inc(a_k[h], 16)

        def a_stats_dve(dve, i):
            for h in range(2):
                ge(dve, a_x[h], i * 16 + 16)
                ge(dve, a_q, i * 8)
                for c in range(NC):
                    nc.vector.bn_stats(stA[:, h * NC + c, :], xa[h][:, c, :]).then_inc(a_st, 1)
                ge(dve, a_st, i * 8 + (h * NC + NC))
                fence(dve)
                for c in range(NC):
                    nc.vector.bn_aggr(mvA[:, h * NC + c, :], stA[:, h * NC + c, :]).then_inc(a_mv, 1)

        def a_dve(dve, i, last=False):
            ge(dve, a_rs, i + 1)
            for h in range(2):
                ge(dve, a_tr, i * 4 + (2 * h - 2))
                for c in range(NC):
                    u = h * NC + c
                    nc.vector.tensor_scalar(qn[u][:, :], xa[h][:, c, :], mvA[:, u, 0:1], rsA[:, u:u + 1],
                                            ALU.subtract, ALU.mult).then_inc(a_q, 1)
            if not last:
                a_stats_dve(dve, i + 1)

        def a_norm_act(act, i):
            ge(act, a_mv, i * 8 + 8)
            nc.scalar.activation(lvA[:, :], mvA[:, :, 1], ACT.Ln, bias=eps_c[:, 0:1]).then_inc(a_lv, 1)
            ge(act, a_lv, i + 1)
            nc.scalar.activation(rsA[:, :], lvA[:, :], ACT.Exp, scale=-0.5).then_inc(a_rs, 1)

        def a_gates_act(act, i, v):
            ge(act, a_gp, i * 4 + (v + 1))
            c0 = 2 * (v % 2)
            dst = gall[:, c0:c0 + 2, :, bass.ds(i * 2 + v // 2, 1), :].rearrange("p c i o h -> p c i (o h)")
            nc.scalar.copy(dst, bank[:, 2 + v % 2, 0:4 * NH].rearrange("p (c i h) -> p c i h", c=2, i=2)).then_inc(a_gs, 1)

        def a_act(act, i, last=False):
            for v in range(4):
                ge(act, a_tr, i * 4 + (v + 1))
                if v % 2 == 0:
                    ge(act, a_qo[v // 2], i * 16)
                nc.scalar.copy(qt[v // 2][:, 2 * (v % 2):2 * (v % 2) + 2, :].rearrange("p c d -> p (c d)"),
                               bank[:, v % 2, :]).then_inc(a_qt, 1)
                if v == 2:
                    a_store(act, i, 0)
                if v:
                    a_gates_act(act, i, v - 1)
                if v == 2 and not last:
                    a_norm_act(act, i + 1)
            a_store(act, i, 1)
            a_gates_act(act, i, 3)

        def a_store(act, i, h):
            ge(act, a_qt, i * 4 + (2 * h + 2))
            act.dma_start(qT_v[:, bass.ds(i * 8 + h * NC, NC), :], qt[h][:, :, :]).then_inc(a_qo[h], 16)

        def a_pe_gates(pe, i, v):
            ge(pe, a_qt, i * 4 + (v + 1))
            ge(pe, a_k[v // 2], i * 16 + 16)
            ge(pe, a_gs, i * 4 + (v - 1))
            for j in range(2):
                c = 2 * (v % 2) + j
                dst = bank[:, 2 + v % 2, j * 2 * NH:(j + 1) * 2 * NH]
                for k in range(KD):
                    nc.tensor.matmul(dst, qt[v // 2][:, c, k * P:(k + 1) * P], wg[:, k, :], start=(k == 0), stop=False)
                for k in range(KD):
                    mm = nc.tensor.matmul(dst, ka[v // 2][:, c, k * P:(k + 1) * P], wgkv[:, k, :],
                                          start=False, stop=(k == KD - 1))
            mm.then_inc(a_gp, 1)

        def a_pe(pe, i):
            for v in range(4):
                ge(pe, a_q, i * 8 + (2 * v + 2))
                ge(pe, a_qt, i * 4 + (v - 1))
                for j in range(2):
                    for k in range(KD):
                        mm = nc.tensor.transpose(bank[:, v % 2, (2 * j + k) * P:(2 * j + k + 1) * P],
                                                 qn[2 * v + j][:, k * P:(k + 1) * P], identf[:, :])
                mm.then_inc(a_tr, 1)
                if v:
                    a_pe_gates(pe, i, v - 1)
            a_pe_gates(pe, i, 3)

        def ends(t):
            return t[:, :].rearrange("p (c s) -> p c s", c=NC)[:, :, P - 1:P]

        def g_actf_all(act):
            act.wait_ge(g_tp, 1)
            nc.scalar.activation(z[:, :], bank[0:BH, 5, :], ACT.Identity, bias=ifb_s[:, 1:2]).then_inc(g_act, 1)
            act.wait_ge(g_dve, 1)
            nc.scalar.activation(g2[:, :], g1[:, :], ACT.Exp).then_inc(g_act, 1)
            act.wait_ge(g_act, 2)
            nc.scalar.activation(g3[:, :], g2[:, :], ACT.Ln, bias=one_c[0:BH, 0:1]).then_inc(g_act, 1)
            act.wait_ge(g_dve, 11)
            nc.scalar.activation(gw[:, :], g1[:, :], ACT.Exp).then_inc(g_act, 1)
            nc.scalar.activation(gE[:, :], g2[:, :], ACT.Exp).then_inc(g_act, 1)
            nc.scalar.activation(gn[:, :], g3[:, :], ACT.Exp, scale=-1.0).then_inc(g_act, 1)
            nc.scalar.activation(gdx[:, :], gd[:, :], ACT.Exp).then_inc(g_act, 1)
            act.wait_ge(g_col, 1)
            for k in range(3):
                src = bank[:, (6, 7, 2)[k], 0:NC * BH].rearrange("p (c b h) -> p b c h", c=NC, b=NB)
                dst = col[:, :, k * NH:(k + 1) * NH].rearrange("p (b c) h -> p b c h", b=NB)
                if k < 2:
                    nc.scalar.copy(dst, src).then_inc(g_cols, 1)
                else:
                    nc.scalar.activation(dst, src, ACT.Identity, bias=neps[:, 0:1]).then_inc(g_cols, 1)
            act.wait_ge(g_dec, 1)
            nc.scalar.copy(col[:, :, 3 * NH:3 * NH + 2].rearrange("p (b c) k -> p b c k", b=NB),
                           bank[:, 3, 0:2 * NB * NC].rearrange("p (b k c) -> p b c k", b=NB, k=2)).then_inc(g_cols, 1)

        def g_pe_all(pe):
            pe.wait_ge(a_gs, NT // 2)
            for k in range(2):
                for c in range(NC):
                    mm = nc.tensor.transpose(bank[0:BH, 4 + k, c * P:(c + 1) * P],
                                             gall[:, c, k, :, :].rearrange("p b h -> p (b h)"), identf[:, :])
            mm.then_inc(g_tp, 1)
            pe.wait_ge(g_act, 7)
            pe.wait_ge(g_spread, 1)
            for k, src in enumerate((gw, gE, gn)):
                for c in range(NC):
                    mm = nc.tensor.transpose(bank[:, (6, 7, 2)[k], c * BH:(c + 1) * BH], src[:, c * P:(c + 1) * P],
                                             identf[0:BH, 0:BH])
            mm.then_inc(g_col, 1)
            for n in range(2 * NB):
                mm = nc.tensor.matmul(bank[:, 3, n * NC:(n + 1) * NC], spread[:, n * P:(n + 1) * P], gdx[:, :], start=True, stop=True)
            mm.then_inc(g_dec, 1)
            pe.wait_ge(g_cols, 4)

        def g_dvef(dve):
            V = nc.vector
            V.tensor_copy(spread[:, :].rearrange("p (b d) -> p b d", d=DH),
                          identf[0:BH, 0:BH].unsqueeze(2).to_broadcast([BH, BH, DH])).then_inc(g_spread, 1)
            dve.wait_ge(g_act, 1)
            V.scalar_tensor_tensor(g1[:, :], z[:, :], -1.0, z[:, :], ALU.mult, ALU.min).then_inc(g_dve, 1)
            dve.wait_ge(g_act, 3)
            V.scalar_tensor_tensor(lf[:, :], z[:, :], 0.0, g3[:, :], ALU.min, ALU.subtract).then_inc(g_dve, 1)
            dve.wait_ge(g_dve, 2)
            V.tensor_tensor_scan(cs[:, :], ones_row[0:BH, :], lf[:, :], 0.0, ALU.mult, ALU.add).then_inc(g_dve, 1)
            dve.wait_ge(g_dve, 3)
            V.scalar_tensor_tensor(ga[:, :], bank[0:BH, 4, :], ifb_s[:, 0:1], cs[:, :], ALU.add,
                                   ALU.subtract).then_inc(g_dve, 1)
            dve.wait_ge(g_dve, 4)
            V.tensor_tensor_scan(gm[:, :], ga[:, :], ga[:, :], -3e38, ALU.max, ALU.max).then_inc(g_dve, 1)
            dve.wait_ge(g_dve, 5)
            c4 = lambda t: t[:, :].rearrange("p (c s) -> p c s", c=NC)
            m_end = ends(gm)
            V.tensor_tensor(c4(g1), c4(ga), m_end.to_broadcast([BH, NC, P]), ALU.subtract).then_inc(g_dve, 1)
            V.memset(g2[:, 0:P], 0.0).then_inc(g_dve, 1)
            V.tensor_tensor(c4(g2)[:, 1:NC, :], m_end[:, 0:NC - 1, :].to_broadcast([BH, NC - 1, P]), c4(gm)[:, 1:NC, :],
                            ALU.subtract).then_inc(g_dve, 1)
            V.tensor_tensor(g3[:, :], cs[:, :], gm[:, :], ALU.add).then_inc(g_dve, 1)
            V.memset(gd[:, 0:1], 0.0).then_inc(g_dve, 1)
            me = c4(gm)[:, :, P - 1]
            V.tensor_tensor(gd[:, 1:NC], me[:, 0:NC - 1], me[:, 1:NC], ALU.subtract).then_inc(g_dve, 1)
            V.tensor_copy(ap[0][:, :], ga[:, :]).then_inc(g_dve, 1)
            V.tensor_scalar(mp[0][:, :], gm[:, :], -1.0, None, ALU.mult).then_inc(g_dve, 1)
            dve.wait_ge(g_dve, 13)
            V.tensor_tensor(r1[:, :], ga[:, :], ap[0][:, :], ALU.subtract).then_inc(g_dve, 1)
            V.scalar_tensor_tensor(r2[:, :], gm[:, :], -1.0, mp[0][:, :], ALU.mult, ALU.subtract).then_inc(g_dve, 1)
            dve.wait_ge(g_dve, 15)
            V.tensor_copy(ap[1][:, :], r1[:, :]).then_inc(g_dve, 1)
            V.tensor_copy(mp[1][:, :], r2[:, :]).then_inc(g_dve, 1)
            dve.wait_ge(g_dve, 17)
            V.tensor_tensor(ap[2][:, :], r1[:, :], ap[1][:, :], ALU.subtract).then_inc(g_dve, 1)
            V.tensor_tensor(mp[2][:, :], r2[:, :], mp[1][:, :], ALU.subtract).then_inc(g_dve, 1)

        def g_sync(sp):
            sp.wait_ge(g_dve, 19)
            for k in range(3):
                for q, part in enumerate((ap[k], mp[k])):
                    sp.dma_start(am_d[:, k * NH:(k + 1) * NH, q, :], part[:, :]).then_inc(g_am, 16)

        HI0 = HG * 2 * DV
        vv = lambda c: kvb[c][:, D:D + NH * DV]

        def b_sync(sp, b, c):
            t = b * NC + c
            ge(sp, b_hs, t - 3)
            ge(sp, b_ut, b * 3 + (c - 2) if c < 3 else b * 3)
            sp.dma_start(kvb[c][:, :], row(kv, t)).then_inc(b_kv[c], 16)
            sp.dma_start(amb[c][:, :, :], am_d[bass.ds(b, 1), :, :, c * P:(c + 1) * P].rearrange(
                "o k x s -> (o k) x s")).then_inc(b_am[c], 16)
            sp.dma_start(qtb[c][:, :], row(qT_d, t)).then_inc(b_q[c], 16)

        def w_sync(sp, b, c):
            t = b * NC + c
            w = c % 2
            ge(sp, w_hi, t - 1)
            ge(sp, w_lo, t - 1)
            sp.dma_start(wst[w][:, :], wts[:, bass.ds(t * WCH, WCH)]).then_inc(w_in[w], 16)

        def w_store(act, b, c):
            t = b * NC + c
            w = c % 2
            ge(act, w_lo, t + 1)
            ge(act, w_hi, t + 1)
            act.dma_start(w_d[:, :, bass.ds(t * WCH, WCH)], whl[w][:, :, :]).then_inc(w_out[w], 16)

        def before(b, c):
            return (b, c - 1) if c else (b - 1, NC - 1)

        def after(b, c):
            return (b, c + 1) if c < NC - 1 else (b + 1, 0)

        def b_scores_pe(pe, b, c):
            t = b * NC + c
            w = c % 2
            for g in range(2):
                n = t * 2 + g
                ge(pe, b_am[c], b * 16 + 16)
                ge(pe, b_D, n - 1)
                dl = bank[:, g, :]
                nc.tensor.matmul(dl, identb[:, :], maskb[:, :].unsqueeze(1).to_broadcast([P, HG, P]),
                                 start=True, stop=False)
                nc.tensor.matmul(dl, amb[c][:, 0, :],
                                 sel24[:, g * HG:(g + 1) * HG].unsqueeze(2).to_broadcast([24, HG, P]),
                                 start=False, stop=False)
                for j in range(HG):
                    mm = nc.tensor.matmul(bank[:, g, j * P:(j + 1) * P],
                                          sel24[:, g * HG + j:g * HG + j + 1].to_broadcast([24, P]), amb[c][:, 1, :],
                                          start=False, stop=(j == HG - 1))
                mm.then_inc(b_dl, 1)
                ge(pe, b_kv[c], b * 16 + 16)
                ge(pe, b_qb, t * HG + HG)
                ge(pe, b_C, n - 1)
                nc.tensor.matmul(bank[:, 2 + g, :], kvb[c][:, g * P:(g + 1) * P],
                                 qbd[w][:, g, :, :].rearrange("p j s -> p (j s)"), start=True, stop=True).then_inc(b_s, 1)

        def b_pe(pe, b, c, mid=None, last=False):
            t = b * NC + c
            if not last:
                b_scores_pe(pe, *after(b, c))
            if mid:
                mid()
            if c < NC - 1:
                ge(pe, b_kw, b * 3 + (c + 1))
                ge(pe, b_ut, b * 3 + c)
                if c == 0:
                    ge(pe, c_lg, b - 1)
                for g in range(2):
                    mm = nc.tensor.matmul(bank[:, 6, g * HG * DV:(g + 1) * HG * DV], kw[c % 2][:, g * P:(g + 1) * P],
                                          vv(c)[:, g * HG * DV:(g + 1) * HG * DV], start=True, stop=True)
                mm.then_inc(b_u, 1)
            ge(pe, b_hs, t)
            if c:
                ge(pe, b_q[c], b * 16 + 16)
                ge(pe, b_st, b * 3 + c)
                for g in range(2):
                    mm = nc.tensor.matmul(bank[:, 4 + g, HI0:HI0 + HG * DV], qtb[c][:, g * P:(g + 1) * P],
                                          St[:, g, :], start=True, stop=True)
                mm.then_inc(b_hi, 1)
            ge(pe, b_vl, t + 1)
            for g in range(2):
                ge(pe, b_Cl, t * 2 + (g + 1))
                k = 2 * (c % 2) + g
                for j in range(HG):
                    hd = g * HG + j
                    nc.tensor.matmul(bank[:, 4 + g, j * 2 * DV:(j + 1) * 2 * DV], Ch[k][:, j * P:(j + 1) * P],
                                     vp[c % 2][:, hd, :, :].rearrange("p k e -> p (k e)"), start=True, stop=False)
                    mm = nc.tensor.matmul(bank[:, 4 + g, j * 2 * DV:j * 2 * DV + DV], Cl[k][:, j * P:(j + 1) * P],
                                          vp[c % 2][:, hd, 0, :], start=False, stop=True)
            mm.then_inc(b_h, 1)

        def b_q_act(act, b, c):
            t = b * NC + c
            w = c % 2
            ge(act, b_q[c], b * 16 + 16)
            ge(act, b_s, t * 2 - 2)
            for j in range(HG):
                rows = slice(DH * j, DH * j + DH)
                nc.scalar.copy(qbd[w][rows, :, j, :], qtb[c][rows, :].rearrange("p (g s) -> p g s", g=2)).then_inc(b_qb, 1)

        def b_exp_act(act, b, c):
            t = b * NC + c
            for g in range(2):
                n = t * 2 + g
                ge(act, b_dl, n + 1)
                ge(act, b_C, n - 1)
                nc.scalar.activation(Dm[g][:, :], bank[:, g, :], ACT.Exp).then_inc(b_D, 1)

        def b_ch_act(act, b, c):
            t = b * NC + c
            ge(act, b_h, t - 1)
            for g in range(2):
                ge(act, b_C, t * 2 + (g + 1))
                nc.scalar.copy(Ch[2 * (c % 2) + g][:, :], Cm[g][:, :]).then_inc(b_Ch, 1)

        def b_act(act, b, c, ahead=2):
            if ahead > 0:
                b_exp_act(act, *after(b, c))
            if ahead > 1:
                b_q_act(act, *after(*after(b, c)))
            w = c % 2
            ge(act, w_in[w], b * 32 + (16 * (c // 2) + 16))
            ge(act, w_out[w], b * 32 + 16 * (c // 2))
            nc.scalar.copy(whl[w][:, 0, :], wst[w][:, :]).then_inc(w_hi, 1)
            if ahead > 0:
                b_ch_act(act, *after(b, c))
            if not (isinstance(b, int) and b == 0 and c == 0):
                w_store(act, *before(b, c))

        def b_kw_pool(pool, b, c):
            t = b * NC + c
            ge(pool, b_ho, t - 3)
            nc.gpsimd.tensor_copy(colb[c][:, :], col[:, bass.ds(t, 1), :].rearrange("p o k -> p (o k)")).then_inc(b_col, 1)
            if c < NC - 1:
                ge(pool, b_col, t + 1)
                ge(pool, b_kv[c], b * 16 + 16)
                ge(pool, b_u, b * 3 + (0, -1, 1)[c])
                vk = vv(c).rearrange("p (h e) -> p h e", e=DV)[:, :, 0:DH]
                nc.gpsimd.tensor_tensor(kw[c % 2][:, :].rearrange("p (h e) -> p h e", e=DH), vk,
                                        colb[c][:, 0:NH].unsqueeze(2).to_broadcast([P, NH, DH]), ALU.mult).then_inc(b_kw, 1)
            ge(pool, b_kv[c], b * 16 + 16)
            ge(pool, b_h, t - 1)
            v3 = vv(c).rearrange("p (h e) -> p h e", e=DV)
            nc.gpsimd.tensor_copy(vp[c % 2][:, :, 0, :], v3).then_inc(b_vh, 1)
            ge(pool, b_vh, t + 1)
            nc.gpsimd.tensor_tensor(vp[c % 2][:, :, 1, :], v3, vp[c % 2][:, :, 0, :], ALU.subtract).then_inc(b_vl, 1)

        def w_pool(pool, b, c):
            t = b * NC + c
            w = c % 2
            ge(pool, w_hi, t + 1)
            ge(pool, w_out[w], b * 32 + 16 * (c // 2))
            nc.gpsimd.tensor_tensor(whl[w][:, 1, :], wst[w][:, :], whl[w][:, 0, :], ALU.subtract).then_inc(w_lo, 1)

        def b_c_dve(dve, b, c):
            t = b * NC + c
            for g in range(2):
                n = t * 2 + g
                ge(dve, b_D, n + 1)
                ge(dve, b_s, n + 1)
                ge(dve, b_Cl, n - 1)
                nc.vector.scalar_tensor_tensor(Cm[g][:, :], bank[:, 2 + g, :], SCALE, Dm[g][:, :], ALU.mult,
                                               ALU.mult).then_inc(b_C, 1)

        def b_cl_dve(dve, b, c):
            t = b * NC + c
            ge(dve, b_h, t - 1)
            for g in range(2):
                k = 2 * (c % 2) + g
                ge(dve, b_Ch, t * 2 + (g + 1))
                nc.vector.tensor_tensor(Cl[k][:, :], Cm[g][:, :], Ch[k][:, :], ALU.subtract).then_inc(b_Cl, 1)

        def b_dve(dve, b, c, mid=None, last=False):
            V = nc.vector
            t = b * NC + c
            if not last:
                b_c_dve(dve, *after(b, c))
            if mid:
                mid(0)
            if not last:
                b_cl_dve(dve, *after(b, c))
            ge(dve, b_col, t + 1)
            if c < NC - 1:
                ge(dve, b_u, b * 3 + (c + 1))
                if c:
                    for g in range(2):
                        V.tensor_scalar(Sd[:, g, :], St[:, g, :], colb[c][:, 3 * NH + g:3 * NH + g + 1], None,
                                        ALU.mult).then_inc(b_sd, 1)
                ub = bank[:, 6, 0:2 * HG * DV].rearrange("p (g e) -> p g e", g=2)
                V.scalar_tensor_tensor(Ut[:, :, :], ub, SCALE, blkm[:, :].unsqueeze(1).to_broadcast([P, 2, HG * DV]),
                                       ALU.mult, ALU.mult).then_inc(b_ut, 1)
                ge(dve, b_ut, b * 3 + (c + 1))
                if c:
                    ge(dve, b_sd, b * 4 + 2 * c)
                    ge(dve, b_hi, b * 3 + c)
                    V.tensor_tensor(St[:, :, :], Sd[:, :, :], Ut[:, :, :], ALU.add).then_inc(b_st, 1)
                else:
                    ge(dve, b_hi, b * 3)
                    V.tensor_copy(St[:, :, :], Ut[:, :, :]).then_inc(b_st, 1)
            ge(dve, b_h, t + 1)
            hp = bank[:, 4:6, 0:HI0].rearrange("p g (h k e) -> p g h k e", k=2, e=DV)
            byg = lambda a: a.rearrange("p (g h) e -> p g h e", g=2)
            if c:
                V.tensor_tensor(byg(t1[:, :, :]), bank[:, 4:6, HI0:HI0 + HG * DV].rearrange("p g (h e) -> p g h e", e=DV),
                                byg(colb[c][:, NH:2 * NH].unsqueeze(2).to_broadcast([P, NH, DV])), ALU.mult).then_inc(b_t1, 1)
                ge(dve, b_t1, b * 3 + c)
                V.tensor_tensor(byg(t2[:, :, :]), hp[:, :, :, 1, :], byg(t1[:, :, :]), ALU.add).then_inc(b_t2, 1)
            else:
                V.tensor_copy(byg(t2[:, :, :]), hp[:, :, :, 1, :]).then_inc(b_t2, 1)
            ge(dve, b_t2, t + 1)
            V.tensor_tensor(byg(Hs[:, :, :]), hp[:, :, :, 0, :], byg(t2[:, :, :]), ALU.add).then_inc(b_hs, 1)
            ge(dve, b_hs, t + 1)
            V.scalar_tensor_tensor(n1[:, :], Hs[:, :, DH], -1.0, Hs[:, :, DH], ALU.mult, ALU.max).then_inc(b_n, 1)
            ge(dve, b_n, t * 3 + 1)
            V.scalar_tensor_tensor(n2[:, :], n1[:, :], N_EPS, colb[c][:, 2 * NH:3 * NH], ALU.add, ALU.max).then_inc(b_n, 1)
            ge(dve, b_n, t * 3 + 2)
            V.reciprocal(n3[:, :], n2[:, :]).then_inc(b_n, 1)
            if mid:
                mid(1)
            ge(dve, b_n, t * 3 + 3)
            if c == 0:
                ge(dve, c_hn, b * 4)
            V.tensor_tensor(h[:, c, :].rearrange("p (h e) -> p h e", e=DH), Hs[:, :, 0:DH],
                            n3[:, :].unsqueeze(2).to_broadcast([P, NH, DH]), ALU.mult).then_inc(b_ho, 1)

        LG0 = 2 * HG * DV

        def c_sync(sp, b):
            ge(sp, c_x2, b)
            sp.dma_start(xc[:, :, :], x_b[bass.ds(b, 1)].rearrange("o p c d -> (o p) c d")).then_inc(c_x, 16)

        def c_dve(dve, b, c, where):
            V = nc.vector
            if c == 0 and where == 0:
                ge(dve, b_ho, b * 4 + 4)
                for k in range(NC):
                    V.bn_stats(st2[:, k, :], h[:, k, :]).then_inc(c_st2, 1)
                ge(dve, c_st2, b * 4 + 4)
                fence(dve)
                for k in range(NC):
                    V.bn_aggr(mv2[:, k, :], st2[:, k, :]).then_inc(c_mv2, 1)
            if c == 0 and where == 1:
                ge(dve, c_rs2, b + 1)
                ge(dve, c_hl, b)
                for k in range(NC):
                    V.tensor_scalar(hn[:, k, :], h[:, k, :], mv2[:, k, 0:1], rs2[:, k:k + 1], ALU.subtract,
                                    ALU.mult).then_inc(c_hn, 1)
            if c == 2 and where == 0:
                ge(dve, c_x2, b + 1)
                for k in range(NC):
                    V.bn_stats(st3[:, k, :], x2[:, k, :]).then_inc(c_st3, 1)
                ge(dve, c_st3, b * 4 + 4)
                fence(dve)
                for k in range(NC):
                    V.bn_aggr(mv3[:, k, :], st3[:, k, :]).then_inc(c_mv3, 1)
            if c == 3 and where == 0:
                ge(dve, c_rs3, b + 1)
                ge(dve, c_yo, b * 16)
                ge(dve, c_yT, b * 2)
                for k in range(NC):
                    V.tensor_scalar(y[:, k, :], x2[:, k, :], mv3[:, k, 0:1], rs3[:, k:k + 1], ALU.subtract,
                                    ALU.mult).then_inc(c_y, 1)

        def c_act(act, b, c):
            if c == 0:
                ge(act, c_mv2, b * 4 + 4)
                nc.scalar.activation(lv2[:, :], mv2[:, :, 1], ACT.Ln, bias=eps_c[:, 0:1]).then_inc(c_lv2, 1)
                ge(act, c_lv2, b + 1)
                nc.scalar.activation(rs2[:, :], lv2[:, :], ACT.Exp, scale=-0.5).then_inc(c_rs2, 1)
            if c == 2:
                ge(act, c_mv3, b * 4 + 4)
                nc.scalar.activation(lv3[:, :], mv3[:, :, 1], ACT.Ln, bias=eps_c[:, 0:1]).then_inc(c_lv3, 1)
                ge(act, c_lv3, b + 1)
                nc.scalar.activation(rs3[:, :], lv3[:, :], ACT.Exp, scale=-0.5).then_inc(c_rs3, 1)
            if c == 3:
                act.dma_start(ov[bass.ds(b, 1)].rearrange("o p c d -> (o p) c d"), x2[:, :, :]).then_inc(c_x2o, 16)
                ge(act, c_y, b * 4 + 4)
                act.dma_start(yv[bass.ds(b, 1), :, :, 0:D].rearrange("o p c d -> (o p) c d"), y[:, :, :]).then_inc(c_yo, 16)
                for k in range(2):
                    ge(act, c_yT, b * 2 + (k + 1))
                    if k == 0:
                        ge(act, c_lp, b)
                    nc.scalar.copy(yT[:, 2 * k:2 * k + 2, :, :].rearrange("p c k t -> p (c k t)"),
                                   bank[:, 7, :]).then_inc(c_yc, 1)

        def c_lg_act(act, b):
            ge(act, c_lp, b + 1)
            nc.scalar.copy(lg[:, bass.ds(b * 4, 4), :].rearrange("p c e -> p (c e)"),
                           bank[:, 6, LG0:LG0 + NC * NE]).then_inc(c_lg, 1)

        def c_pool(pool, b, c):
            if c == 1:
                ge(pool, c_hn, b * 4 + 4)
                ge(pool, c_x, b * 16 + 16)
                nc.gpsimd.tensor_tensor(hl[:, :, :], hn[:, :, :], lsg[:, :].unsqueeze(1).to_broadcast([P, NC, D]),
                                        ALU.mult).then_inc(c_hl, 1)
                ge(pool, c_hl, b + 1)
                ge(pool, c_y, b * 4)
                ge(pool, c_x2o, b * 16)
                nc.gpsimd.tensor_tensor(x2[:, :, :], hl[:, :, :], xc[:, :, :], ALU.add).then_inc(c_x2, 1)

        def c_pe(pe, b, c):
            if c == 3:
                for k in range(2):
                    ge(pe, c_y, b * 4 + (2 * k + 2))
                    ge(pe, c_yc, b * 2 + k)
                    for j in range(4):
                        mm = nc.tensor.transpose(bank[:, 7, j * P:(j + 1) * P],
                                                 y[:, 2 * k + j // 2, (j % 2) * P:(j % 2 + 1) * P], identf[:, :])
                    mm.then_inc(c_yT, 1)

        def c_pe2(pe, b, states):
            ge(pe, c_yc, b * 2 + 2)
            ge(pe, b_ut, states)
            ge(pe, c_lg, b)
            for k in range(NC):
                for j in range(KD):
                    mm = nc.tensor.matmul(bank[:, 6, LG0 + k * NE:LG0 + (k + 1) * NE], yT[:, k, j, :], wr[:, j, :],
                                          start=(j == 0), stop=(j == KD - 1))
            mm.then_inc(c_lp, 1)

        V_ = sb("topv", [P, NT, 8]); I_ = sb("topi", [P, NT, 8], U32)
        zr = sb("zr", [P, NT, NE]); er = sb("er", [P, NT, NE]); sc = sb("sc", [P, NT, NE]); sr = sb("sr", [P, NT, NE])
        den = sb("den", [P, NT]); rd = sb("rd", [P, NT]); ck = sb("ck", [P, 2, NT]); ik = sb("ik", [P, 2, NT])
        Mk = sb("Mk", [P, 2, NE, NT]); Mb = sb("Mb", [P, NE, NT], BF16)
        cwm = sb("cwm", [P, 2, NT, NE]); cw16 = sb("cw16", [P, NT, 16])
        tot = sb("tot", [P, NE, NT]); Ci = sb("Ci", [P, NE, NT]); Cx = sb("Cx", [P, NE, NT]); pos = sb("pos", [P, NE, NT])
        pos2 = sb("pos2", [P, NE, NT])
        ne_ = sb("ne_", [P, NE]); nei = sb("nei", [P, NE], I32); nsi = sb("nsi", [P, NE], I32); nsl = sb("nsl", [P, NE])
        SBi = sb("SBi", [P, NE]); SBx = sb("SBx", [P, NE]); off = sb("off", [P, NE])
        pk = sb("pk", [P, 2, NE, NT]); pk1 = sb("pk1", [P, 2, NT]); pki = sb("pki", [P, 2, NT], I32)
        qki = sb("qki", [P, 2, NT], I32); qk = sb("qk", [P, 2, NT]); rk = sb("rk", [P, 2, NT])
        sle = sb("sle", [P, SLOTS, NE]); esl = sb("esl", [P, SLOTS]); eoff = sb("eoff", [1, SLOTS], I32)
        esm = sb("esm", [P, SLOTS])
        R_ = [sb(f"R{k}", [P, P]) for k in range(4)]; Q_ = [sb(f"Q{k}", [P, NQ]) for k in range(4)]
        TAB = sb("TAB", [P, SLOTS, 4 + NE]); tA = sb("tA", [P, NQ])
        r_ch = sem("r_ch"); r_act = sem("r_act"); r_mb = sem("r_mb"); r_rk = sem("r_rk"); r_cw = sem("r_cw")
        r_cwo = sem("r_cwo"); r_eoff = sem("r_eoff"); r_R = sem("r_R"); r_Q = sem("r_Q"); r_mm = sem("r_mm")
        r_tab = sem("r_tab")

        def r_dve(dve):
            V = nc.vector
            n = [0]

            def step(ins):
                n[0] += 1
                ins.then_inc(r_ch, 1)
                dve.wait_ge(r_ch, n[0])

            dve.wait_ge(c_lg, NB)
            V.tensor_tensor(zr[:, :, :], lg[:, :, :], rb[:, :].unsqueeze(1).to_broadcast([P, NT, NE]), ALU.add).then_inc(r_act, 1)
            dve.wait_ge(r_act, 2)
            step(V.tensor_scalar(sr[:, :, :], er[:, :, :], 1.0, None, ALU.add))
            step(V.reciprocal(sc[:, :, :], sr[:, :, :]))
            for t in range(NT):
                ins = V.max(V_[:, t, :], sc[:, t, :])
            step(ins)
            for t in range(NT):
                ins = V.max_index(I_[:, t, :], V_[:, t, :], sc[:, t, :])
            step(ins)
            v12 = V_[:, :, 0:2].rearrange("p t k -> p k t")
            step(V.tensor_copy(ik[:, :, :], I_[:, :, 0:2].rearrange("p t k -> p k t")))
            step(V.scalar_tensor_tensor(den[:, :], V_[:, :, 0], TOP_EPS, V_[:, :, 1], ALU.add, ALU.add))
            step(V.reciprocal(rd[:, :], den[:, :]))
            step(V.scalar_tensor_tensor(ck[:, :, :], v12, tg[:, 1:2], rd[:, :].unsqueeze(1).to_broadcast([P, 2, NT]),
                                        ALU.mult, ALU.mult))
            e_of = rowj[:, 0:NE].unsqueeze(2).to_broadcast([P, NE, NT])
            for k in range(2):
                step(V.tensor_tensor(Mk[:, k, :, :], ik[:, k, :].unsqueeze(1).to_broadcast([P, NE, NT]), e_of, ALU.is_equal))
            V.tensor_tensor(Mb[:, :, :], Mk[:, 0, :, :], Mk[:, 1, :, :], ALU.add).then_inc(r_mb, 1)
            for k in range(2):
                step(V.tensor_tensor(cwm[:, k, :, :], Mk[:, k, :, :].rearrange("p e t -> p t e"),
                                     ck[:, k, :].unsqueeze(2).to_broadcast([P, NT, NE]), ALU.mult))
            V.memset(cw16[:, :, NE:16], 0.0).then_inc(r_cw, 1)
            V.tensor_tensor(cw16[:, :, 0:NE], cwm[:, 0, :, :], cwm[:, 1, :, :], ALU.add).then_inc(r_cw, 1)
            dve.wait_ge(r_rk, 2)
            totp = bank[:, 1, 0:NE * NT]
            step(V.tensor_copy(tot[:, :, :].rearrange("p e t -> p (e t)"), totp))
            step(V.tensor_tensor_scan(Ci[:, :, :].rearrange("p e t -> p (e t)"), ones_row[:, 0:NE * NT],
                                      tot[:, :, :].rearrange("p e t -> p (e t)"), 0.0, ALU.mult, ALU.add))
            step(V.tensor_tensor(Cx[:, :, :], Ci[:, :, :], tot[:, :, :], ALU.subtract))
            step(V.tensor_tensor(ne_[:, :], Ci[:, :, NT - 1], Cx[:, :, 0], ALU.subtract))
            step(V.tensor_scalar(nei[:, :], ne_[:, :], float(SLOT - 1), None, ALU.add))
            step(V.tensor_scalar(nsi[:, :], nei[:, :], 8, None, ALU.arith_shift_right))
            step(V.tensor_copy(nsl[:, :], nsi[:, :]))
            step(V.tensor_tensor_scan(SBi[:, :], ones_row[:, 0:NE], nsl[:, :], 0.0, ALU.mult, ALU.add))
            step(V.tensor_tensor(SBx[:, :], SBi[:, :], nsl[:, :], ALU.subtract))
            step(V.scalar_tensor_tensor(off[:, :], SBx[:, :], float(SLOT), Cx[:, :, 0], ALU.mult, ALU.subtract))
            step(V.tensor_tensor(pos[:, :, :].rearrange("p e t -> p (e t)"), bank[:, 0, 0:NE * NT],
                                 Cx[:, :, :].rearrange("p e t -> p (e t)"), ALU.add))
            step(V.tensor_tensor(pos2[:, :, :], pos[:, :, :], off[:, :].unsqueeze(2).to_broadcast([P, NE, NT]), ALU.add))
            for k in range(2):
                step(V.tensor_tensor(pk[:, k, :, :], Mk[:, k, :, :], pos2[:, :, :], ALU.mult))
                step(V.tensor_reduce(pk1[:, k, :], pk[:, k, :, :].rearrange("p e t -> p t e"), AX.X, ALU.add))
            step(V.tensor_copy(pki[:, :, :], pk1[:, :, :]))
            step(V.tensor_scalar(qki[:, :, :], pki[:, :, :], 7, None, ALU.arith_shift_right))
            step(V.tensor_copy(qk[:, :, :], qki[:, :, :]))
            step(V.scalar_tensor_tensor(rk[:, :, :], qk[:, :, :], -float(P), pk1[:, :, :], ALU.mult, ALU.add))
            step(V.tensor_tensor(sle[:, :, :], SBi[:, :].unsqueeze(1).to_broadcast([P, SLOTS, NE]),
                                 rowj[:, 0:SLOTS].unsqueeze(2).to_broadcast([P, SLOTS, NE]), ALU.is_le))
            step(V.tensor_reduce(esl[:, :], sle[:, :, :], AX.X, ALU.add))
            step(V.tensor_scalar(esm[:, :], esl[:, :], float(NE - 1), None, ALU.min))
            V.tensor_scalar(eoff[:, :], esm[0:1, :], float(WE), None, ALU.mult).then_inc(r_eoff, 1)
            V.tensor_tensor(TAB[:, :, 4:4 + NE], esm[:, :].unsqueeze(2).to_broadcast([P, SLOTS, NE]),
                            rowj[:, 0:NE].unsqueeze(1).to_broadcast([P, SLOTS, NE]), ALU.is_equal).then_inc(r_tab, 1)

        def r_onehot_dve(dve, i):
            V = nc.vector
            for u in range(4):
                t, k = i * 2 + u // 2, u % 2
                ge(dve, r_mm, i * 4 + (u - 3))
                V.tensor_scalar(R_[u][:, :], rowj[:, :], rk[:, k, bass.ds(t, 1)], None, ALU.is_equal).then_inc(r_R, 1)
                V.tensor_scalar(Q_[u][:, :], rowj[:, 0:NQ], qk[:, k, bass.ds(t, 1)], tokp1[:, bass.ds(t, 1)],
                                ALU.is_equal, ALU.mult).then_inc(r_Q, 1)

        def r_onehot_pe(pe, i, first=False, last=False):
            for u in range(4):
                ge(pe, r_R, i * 4 + (u + 1))
                ge(pe, r_Q, i * 4 + (u + 1))
                nc.tensor.matmul(bank[:, 2, 0:NQ], R_[u][:, :], Q_[u][:, :], start=(first and u == 0),
                                 stop=(last and u == 3)).then_inc(r_mm, 1)

        def r_tab_dve(dve):
            V = nc.vector
            dve.wait_ge(r_mm, 2 * NT)
            T1 = bank[:, 2, 0:NQ]
            V.tensor_scalar(tA[:, :], T1, 0.0, SKIP, ALU.is_equal, ALU.mult).then_inc(r_tab, 1)
            V.tensor_scalar(TAB[:, :, 0:2], T1.rearrange("p (s j) -> p s j", j=2), -1.0, 0.0, ALU.add,
                            ALU.max).then_inc(r_tab, 1)
            dve.wait_ge(r_tab, 3)
            V.scalar_tensor_tensor(TAB[:, :, 2:4], T1.rearrange("p (s j) -> p s j", j=2), -1.0,
                                   tA[:, :].rearrange("p (s j) -> p s j", j=2), ALU.add, ALU.add).then_inc(r_tab, 1)

        w13 = [sb(f"w13_{w}", [P, 2, W13], BF16) for w in range(2)]
        w2_ = [sb(f"w2_{w}", [P, 2, W2C], BF16) for w in range(2)]
        gid = [sb(f"gid{w}", [P, 2], I32) for w in range(2)]
        sid = [sb(f"sid{w}", [P, 2], I32) for w in range(2)]
        xg = [sb(f"xg{w}", [P, 2, YW]) for w in range(2)]
        xh = [sb(f"xh{w}", [P, KD, SLOT], BF16) for w in range(2)]
        xl = [sb(f"xl{w}", [P, KD, SLOT], BF16) for w in range(2)]
        hh = [sb(f"hh{w}", [P, NM, SLOT], BF16) for w in range(2)]
        hl_ = [sb(f"hlo{w}", [P, NM, SLOT], BF16) for w in range(2)]
        sg = [sb(f"sg{w}", [P, SLOT]) for w in range(2)]
        hf = [sb(f"hf{w}", [P, SLOT]) for w in range(3)]
        cwt = [sb(f"cwt{w}", [P, 2, NE]) for w in range(2)]
        cws = [sb(f"cws{w}", [P, 2]) for w in range(2)]
        res = [sb(f"res{w}", [P, 2, D]) for w in range(2)]
        f_w1 = [sem(f"f_w1{w}") for w in range(2)]; f_w2 = [sem(f"f_w2{w}") for w in range(2)]; f_gid = sem("f_gid"); f_xg = [sem(f"f_xg{w}") for w in range(2)]
        f_T = sem("f_T"); f_xh = sem("f_xh"); f_xl = sem("f_xl"); f_l1 = sem("f_l1"); f_sg = sem("f_sg")
        f_hf = sem("f_hf"); f_hh = sem("f_hh"); f_hl = sem("f_hl"); f_y = sem("f_y"); f_cwt = sem("f_cwt")
        f_cws = sem("f_cws"); f_res = sem("f_res"); f_sid = sem("f_sid"); f_out = sem("f_out")

        def f_sync(sp, s, w):
            e = sp.value_load(eoff[0:1, bass.ds(s, 1)], min_val=0, max_val=(NE - 1) * WE)
            ge(sp, f_l1, s * NM - NM)
            sp.dma_start(w13[w][:, :, :], w_d[:, :, bass.ds(e, W13)]).then_inc(f_w1[w], 16)
            ge(sp, f_y, s - 1)
            sp.dma_start(w2_[w][:, :, :], w_d[:, :, bass.ds(e + W13, W2C)]).then_inc(f_w2[w], 16)

        def f_gather(pool, s, sh, w):
            ge(pool, f_T, s - 1)
            ge(pool, f_cwt, s - 1)
            nc.gpsimd.tensor_copy(gid[w][:, :], TAB[:, bass.ds(s, 1), 0:2].rearrange("p o k -> p (o k)")).then_inc(f_gid, 1)
            ge(pool, f_gid, s + 1)
            for j in range(2):
                nc.gpsimd.indirect_dma_start(xg[w][:, j, :], None, y_d,
                                             bass.IndirectOffsetOnAxis(ap=gid[w][:, j:j + 1], axis=0)).then_inc(f_xg[w], 16)

        def f_scatter(pool, s, w):
            ge(pool, f_out, s * 32)
            nc.gpsimd.tensor_copy(sid[w][:, :], TAB[:, bass.ds(s, 1), 2:4].rearrange("p o k -> p (o k)")).then_inc(f_sid, 1)
            ge(pool, f_sid, s + 1)
            ge(pool, f_res, s * 2 + 2)
            for j in range(2):
                if j:
                    ge(pool, f_out, s * 32 + 16)
                nc.gpsimd.indirect_dma_start(out, bass.IndirectOffsetOnAxis(ap=sid[w][:, j:j + 1], axis=0),
                                             res[w][:, j, :], None, bounds_check=TOK - 1, oob_is_err=False,
                                             compute_op=ALU.add).then_inc(f_out, 16)

        XT = lambda w: bank[:, w, :].rearrange("p (k t) -> p k t", k=KD)

        def f_T_pe(pe, s, sh, w):
            ge(pe, f_xg[w], sh * 32 + 32)
            ge(pe, f_xl, s - 1)
            for j in range(2):
                for k in range(KD):
                    mm = nc.tensor.transpose(XT(w)[:, k, j * P:(j + 1) * P], xg[w][:, j, k * P:(k + 1) * P], identf[:, :])
            mm.then_inc(f_T, 1)

        def three(dst, pairs):
            for n, (l, r) in enumerate(pairs):
                mm = nc.tensor.matmul(dst, l, r, start=(n == 0), stop=(n == len(pairs) - 1))
            return mm

        def f_l1_pe(pe, s, sh, w):
            ge(pe, f_w1[w], sh * 16 + 16)
            ge(pe, f_xh, s + 1)
            ge(pe, f_xl, s + 1)
            for m in range(NM):
                n = s * NM + m
                ge(pe, f_hf, n - 3)
                bk = 2 + (NM * w + m) % 4
                for q in range(2 if m < NM - 1 else 1):
                    pairs = []
                    for k in range(KD):
                        c0 = k * 2 * HID + (2 * m + q) * P
                        H_, L_ = w13[w][:, 0, c0:c0 + P], w13[w][:, 1, c0:c0 + P]
                        pairs += [(H_, xh[w][:, k, :]), (H_, xl[w][:, k, :]), (L_, xh[w][:, k, :])]
                    mm = three(bank[:, bk, q * SLOT:(q + 1) * SLOT], pairs)
                mm.then_inc(f_l1, 1)

        def f_l2_pe(pe, s, sh, w):
            ge(pe, f_w2[w], sh * 16 + 16)
            ge(pe, f_hh, s * NM + NM)
            ge(pe, f_hl, s * NM + NM)
            ge(pe, f_res, s * 2 - 2)
            for j in range(2):
                pairs = []
                for m in range(NM):
                    K = P if m < NM - 1 else HREM
                    c0 = m * D
                    hi, lo = hh[w][0:K, m, j * P:(j + 1) * P], hl_[w][0:K, m, j * P:(j + 1) * P]
                    wh, wl = w2_[w][0:K, 0, c0:c0 + D], w2_[w][0:K, 1, c0:c0 + D]
                    pairs += [(hi, wh), (hi, wl), (lo, wh)]
                mm = three(bank[:, 6 + w, j * D:(j + 1) * D], pairs)
            mm.then_inc(f_y, 1)

        def f_x_act(act, s, w):
            ge(act, f_T, s + 1)
            ge(act, f_l1, s * NM - NM)
            nc.scalar.copy(xh[w][:, :, :], XT(w)).then_inc(f_xh, 1)

        def f_x_dve(dve, s, sh, w):
            V = nc.vector
            ge(dve, f_xg[w], sh * 32 + 32)
            ge(dve, f_cws, s - 1)
            V.tensor_tensor(cwt[w][:, :, :], xg[w][:, :, D:D + NE],
                            TAB[:, bass.ds(s, 1), 4:4 + NE].to_broadcast([P, 2, NE]), ALU.mult).then_inc(f_cwt, 1)
            ge(dve, f_xh, s + 1)
            ge(dve, f_l1, s * NM - NM)
            V.tensor_tensor(xl[w][:, :, :], XT(w), xh[w][:, :, :], ALU.subtract).then_inc(f_xl, 1)

        def f_h_act(act, s, w):
            def hi(m):
                K = P if m < NM - 1 else HREM
                n = s * NM + m
                ge(act, f_hf, n + 1)
                if m == 0:
                    ge(act, f_y, s - 1)
                nc.scalar.copy(hh[w][0:K, m, :], hf[m % 3][0:K, :]).then_inc(f_hh, 1)
            for m in range(NM):
                K = P if m < NM - 1 else HREM
                n = s * NM + m
                ge(act, f_l1, n + 1)
                ge(act, f_hf, n - 1)
                nc.scalar.activation(sg[m % 2][0:K, :], bank[0:K, 2 + (NM * w + m) % 4, 0:SLOT], ACT.Silu).then_inc(f_sg, 1)
                if m:
                    hi(m - 1)
            hi(NM - 1)

        def f_h_dve(dve, s, w):
            V = nc.vector

            def lo(m):
                K = P if m < NM - 1 else HREM
                n = s * NM + m
                ge(dve, f_hh, n + 1)
                if m == 0:
                    ge(dve, f_y, s - 1)
                V.tensor_tensor(hl_[w][0:K, m, :], hf[m % 3][0:K, :], hh[w][0:K, m, :], ALU.subtract).then_inc(f_hl, 1)
            ge(dve, f_cwt, s + 1)
            ge(dve, f_res, s * 2 - 2)
            V.tensor_reduce(cws[w][:, :], cwt[w][:, :, :], AX.X, ALU.add).then_inc(f_cws, 1)
            for m in range(NM):
                n = s * NM + m
                ge(dve, f_sg, n + 1)
                ge(dve, f_hl, n - 2)
                ge(dve, f_hh, n - 2)
                bk = 2 + (NM * w + m) % 4
                if m < NM - 1:
                    V.tensor_tensor(hf[m % 3][:, :], sg[m % 2][:, :], bank[:, bk, SLOT:2 * SLOT], ALU.mult).then_inc(f_hf, 1)
                else:
                    V.tensor_tensor(hf[m % 3][0:HREM, :], sg[m % 2][0:HREM, :], bank[HREM:P, bk, 0:SLOT],
                                    ALU.mult).then_inc(f_hf, 1)
                if m:
                    lo(m - 1)
            lo(NM - 1)

        def f_e_dve(dve, s, w):
            ge(dve, f_y, s + 1)
            ge(dve, f_cws, s + 1)
            ge(dve, f_out, s * 32 - 32)
            for j in range(2):
                nc.vector.tensor_scalar(res[w][:, j, :], bank[:, 6 + w, j * D:(j + 1) * D], cws[w][:, j:j + 1], None,
                                        ALU.mult).then_inc(f_res, 1)

        def f_pe(pe, s, sh, w, t_next=True, prev=True):
            f_l1_pe(pe, s, sh, w)
            if t_next:
                f_T_pe(pe, s + 1, sh + w, 1 - w)
            if prev:
                f_l2_pe(pe, s - 1, sh - 1 + w, 1 - w)

        def f_act(act, s, sh, w, t_next=True, prev=True):
            f_h_act(act, s, w)
            if t_next:
                f_x_act(act, s + 1, 1 - w)

        def f_dve(dve, s, sh, w, t_next=True, prev=True):
            f_h_dve(dve, s, w)
            if t_next:
                f_x_dve(dve, s + 1, sh + w, 1 - w)
            if prev:
                f_e_dve(dve, s - 1, 1 - w)

        def slots(eng, step):
            step(eng, 0, 0, 0, True, False)
            for s in range(1, 4):
                step(eng, s, s // 2, s % 2)
            with eng.Fori(2, SLOTS // 2 - 1) as i:
                for w in range(2):
                    step(eng, i * 2 + w, i, w)
            step(eng, SLOTS - 2, SLOTS // 2 - 1, 0)
            step(eng, SLOTS - 1, SLOTS // 2 - 1, 1, False, True)

        block = ctx.enter_context(nc.Block())

        @block.sync
        def _(sp):
            a_x_sync(sp, 0)
            sp.dma_start(wg[:, :, :], wgate).then_inc(s_small, 16)
            sp.dma_start(ifb_s[:, :], ifb).then_inc(s_small, 16)
            sp.dma_start(lnr[:, :], lnrow).then_inc(s_small, 16)
            sp.dma_start(gs[:, :], gsc).then_inc(s_small, 16)
            sp.dma_start(wr[:, :, :], wroute).then_inc(s_small, 16)
            sp.dma_start(rb[:, :], rbias).then_inc(s_small, 16)
            a_k_sync(sp, 0)
            with sp.Fori(1, NT // 8) as i:
                a_x_sync(sp, i)
                a_k_sync(sp, i)
            g_sync(sp)
            sp.wait_ge(g_am, 16 * 6)
            for h in range(2):
                sp.wait_ge(a_qo[h], 16 * NT // 8)
            b_sync(sp, 0, 0)
            for c in range(NC):
                b_sync(sp, *after(0, c))
                w_sync(sp, 0, c)

            def batch(b, last=False):
                for c in range(NC):
                    if c == 0:
                        c_sync(sp, b - 1)
                    if not (last and c == NC - 1):
                        b_sync(sp, *after(b, c))
                    w_sync(sp, b, c)

            batch(1)
            with sp.Fori(2, NB - 1) as b:
                batch(b)
            batch(NB - 1, last=True)
            c_sync(sp, NB - 1)
            for w in range(2):
                sp.wait_ge(w_out[w], 16 * NT // 2)
            sp.wait_ge(r_eoff, 1)
            for s in range(4):
                f_sync(sp, s, s % 2)
            with sp.Fori(2, SLOTS // 2) as i:
                for w in range(2):
                    f_sync(sp, i * 2 + w, w)

        @block.scalar
        def _(act):
            act.wait_ge(s_const, NCONST)
            a_norm_act(act, 0)
            consts_act(act)
            a_act(act, 0)
            with act.Fori(1, NT // 8 - 1) as i:
                a_act(act, i)
            a_act(act, NT // 8 - 1, last=True)
            g_actf_all(act)
            act.wait_ge(s_qz, 2)
            b_q_act(act, 0, 0)
            b_exp_act(act, 0, 0)
            b_q_act(act, 0, 1)
            b_ch_act(act, 0, 0)
            for c in range(NC):
                b_act(act, 0, c)

            def batch(b, last=False):
                for c in range(NC):
                    if c == 0 and not (isinstance(b, int) and b < 2):
                        c_lg_act(act, b - 2)
                    b_act(act, b, c, min(2, NC - 1 - c) if last else 2)
                    c_act(act, b - 1, c)

            batch(1)
            with act.Fori(2, NB - 1) as b:
                batch(b)
            batch(NB - 1, last=True)
            w_store(act, NB - 1, NC - 1)
            c_lg_act(act, NB - 2)
            for c in range(NC):
                c_act(act, NB - 1, c)
            c_lg_act(act, NB - 1)
            act.wait_ge(r_act, 1)
            nc.scalar.activation(er[:, :, :], zr[:, :, :], ACT.Exp, scale=-1.0).then_inc(r_act, 1)
            act.wait_ge(r_cw, 2)
            act.wait_ge(c_yo, 16 * NB)
            act.dma_start(y_d[:, D:YW].rearrange("(t p) e -> p t e", p=P), cw16[:, :, :]).then_inc(r_cwo, 16)
            f_x_act(act, 0, 0)
            slots(act, f_act)

        @block.vector
        def _(dve):
            consts_dve(dve)
            a_stats_dve(dve, 0)
            wgkv_dve(dve)
            a_dve(dve, 0)
            with dve.Fori(1, NT // 8 - 1) as i:
                a_dve(dve, i)
            a_dve(dve, NT // 8 - 1, last=True)
            lsg_dve(dve)
            g_dvef(dve)
            b_c_dve(dve, 0, 0)
            b_cl_dve(dve, 0, 0)
            for c in range(NC):
                b_dve(dve, 0, c)

            def batch(b, last=False):
                for c in range(NC):
                    b_dve(dve, b, c, mid=lambda where: c_dve(dve, b - 1, c, where), last=last and c == NC - 1)

            batch(1)
            with dve.Fori(2, NB - 1) as b:
                batch(b)
            batch(NB - 1, last=True)
            for c in range(NC):
                for where in range(2):
                    c_dve(dve, NB - 1, c, where)
            r_dve(dve)
            r_onehot_dve(dve, 0)
            with dve.Fori(1, NT // 2) as i:
                r_onehot_dve(dve, i)
            r_tab_dve(dve)
            f_x_dve(dve, 0, 0, 0)
            slots(dve, f_dve)
            f_e_dve(dve, SLOTS - 1, 1)

        @block.gpsimd
        def _(pool):
            consts_pool(pool)
            pool.wait_ge(s_lsg, 1)
            pool.wait_ge(g_cols, 4)
            b_kw_pool(pool, 0, 0)
            for c in range(NC):
                b_kw_pool(pool, *after(0, c))
                w_pool(pool, 0, c)

            def batch(b, last=False):
                for c in range(NC):
                    if not (last and c == NC - 1):
                        b_kw_pool(pool, *after(b, c))
                    c_pool(pool, b - 1, c)
                    w_pool(pool, b, c)

            batch(1)
            with pool.Fori(2, NB - 1) as b:
                batch(b)
            batch(NB - 1, last=True)
            c_pool(pool, NB - 1, 1)
            pool.wait_ge(r_tab, 4)
            pool.wait_ge(r_cwo, 16)
            pool.wait_ge(c_x2o, 16 * NB)
            f_gather(pool, 0, 0, 0)
            f_gather(pool, 1, 0, 1)
            f_gather(pool, 2, 1, 0)

            def rows_in_out(i):
                f_gather(pool, i * 2 + 1, i, 1)
                f_scatter(pool, i * 2 - 2, 0)
                f_gather(pool, i * 2 + 2, i + 1, 0)
                f_scatter(pool, i * 2 - 1, 1)

            rows_in_out(1)
            with pool.Fori(2, SLOTS // 2 - 1) as i:
                rows_in_out(i)
            f_gather(pool, SLOTS - 1, SLOTS // 2 - 1, 1)
            for s in range(SLOTS - 4, SLOTS):
                f_scatter(pool, s, s % 2)
            pool.wait_ge(f_out, 32 * SLOTS)

        @block.tensor
        def _(pe):
            pe.wait_ge(s_const, NCONST)
            pe.wait_ge(s_wgkv, 1)
            a_pe(pe, 0)
            with pe.Fori(1, NT // 8) as i:
                a_pe(pe, i)
            g_pe_all(pe)
            b_scores_pe(pe, 0, 0)
            for c in range(NC):
                b_pe(pe, 0, c)

            def batch(b, last=False):
                for c in range(NC):
                    b_pe(pe, b, c, mid=lambda: c_pe(pe, b - 1, c), last=last and c == NC - 1)
                    if c == 3:
                        c_pe2(pe, b - 1, b * 3 + 3)

            batch(1)
            with pe.Fori(2, NB - 1) as b:
                batch(b)
            batch(NB - 1, last=True)
            c_pe(pe, NB - 1, 3)
            c_pe2(pe, NB - 1, NB * 3)
            pe.wait_ge(r_mb, 1)
            mb = Mb[:, :, :].rearrange("p e t -> p (e t)")
            nc.tensor.matmul(bank[:, 0, 0:NE * NT], upperb[:, :], mb, start=True, stop=True).then_inc(r_rk, 1)
            nc.tensor.matmul(bank[:, 1, 0:NE * NT], onesb[:, :], mb, start=True, stop=True).then_inc(r_rk, 1)
            r_onehot_pe(pe, 0, first=True)
            with pe.Fori(1, NT // 2 - 1) as i:
                r_onehot_pe(pe, i)
            r_onehot_pe(pe, NT // 2 - 1, last=True)
            f_T_pe(pe, 0, 0, 0)
            slots(pe, f_pe)
            f_l2_pe(pe, SLOTS - 1, SLOTS // 2 - 1, 1)



_IN = ['x', 'kv', 'wgate', 'ifb', 'lnrow', 'gsc', 'wroute', 'rbias', 'wts']


def layout(i):
    import numpy as np
    a = {k: np.asarray(v) for k, v in i.items()}
    x = a['x'].reshape(TOK, D)
    ctx = a['ctx_1024'].reshape(NT, P, D)
    kT = ctx.transpose(0, 2, 1).reshape(NT, KD, P, P).transpose(0, 2, 1, 3).reshape(NT, P, D)
    v = np.concatenate([ctx.reshape(NT, P, NH, DH), np.ones((NT, P, NH, 1), np.float32)], -1).reshape(NT, P, NH * DV)
    kv = np.concatenate([kT, v], -1)
    gw = np.concatenate([a['L0_xattn_igate_w'], a['L0_xattn_fgate_w']], 0).T
    wgate = gw.reshape(6, P, 2 * NH).transpose(1, 0, 2)
    ifb = np.stack([np.tile(a['L0_xattn_igate_b'], NB), np.tile(a['L0_xattn_fgate_b'], NB)], 1)
    lnrow = np.tile(a['L0_xattn_ln_scale'][None], (P, 1))
    gsc = np.tile(np.stack([a['g_xattn'][0], a['g_ffn'][0]])[None], (P, 1))
    gate = np.concatenate([a['L0_ffn_gate_weight'], a['L0_ffn_new_gate_weight']], 0).T
    wroute = gate.reshape(KD, P, NE).transpose(1, 0, 2)
    rbias = np.tile(np.concatenate([np.zeros(NE - 1, np.float32), a['L0_ffn_gate_bias']])[None], (P, 1))
    cat = lambda n: np.concatenate([a[f'L0_ffn_{n}'], a[f'L0_ffn_new_{n}']], 0)
    w1, w3 = (cat(n).transpose(0, 2, 1) for n in ('w1', 'w3'))
    full = (NM - 1) * P
    m13 = np.stack([w1[:, :, :full].reshape(NE, D, NM - 1, P), w3[:, :, :full].reshape(NE, D, NM - 1, P)], 3)
    w13 = np.concatenate([m13.reshape(NE, D, 2 * full), w1[:, :, full:], w3[:, :, full:]], -1)
    w13 = w13.reshape(NE, KD, P, 2 * HID).transpose(2, 0, 1, 3).reshape(P, NE, W13)
    w2 = cat('w2').transpose(0, 2, 1)
    w2 = np.concatenate([w2, np.zeros((NE, NM * P - HID, D), np.float32)], 1)
    w2 = w2.reshape(NE, NM, P, D).transpose(2, 0, 1, 3).reshape(P, NE, W2C)
    wts = np.concatenate([w13, w2], -1).reshape(P, WALL)
    made = dict(x=x, kv=kv, wgate=wgate, ifb=ifb, lnrow=lnrow, gsc=gsc, wroute=wroute, rbias=rbias, wts=wts)
    return {k: np.ascontiguousarray(v) for k, v in made.items()}


def kernel(**inputs):
    import concourse.bacc as _bacc
    from concourse import mybir as _mybir
    from concourse.bass_utils import run_bass_kernel_spmd as _run

    nc = _bacc.Bacc("TRN2", target_bir_lowering=False, num_devices=1)
    made = layout(inputs)
    arrays, args = {}, []
    for name in _IN:
        v = made[name]
        arrays[f"in_{name}"] = v
        args.append(nc.dram_tensor(f"in_{name}", v.shape, _mybir.dt.from_np(v.dtype), kind="ExternalInput").ap())
    args.append(nc.dram_tensor("out_0", (TOK, D), _mybir.dt.float32, kind="ExternalOutput").ap())
    build(nc, *args)
    r = _run(nc, [arrays], core_ids=[0])
    return r.results[0]["out_0"].reshape(NB, S, D)
```
